# Optimizing a Trainium2 kernel written in Bass

```python
import numpy as np
import jax
import jax.numpy as jnp

def _softmax(x, axis=-1):
    return jax.nn.softmax(x, axis=axis)

def _gelu(x):
    return jax.nn.gelu(x, approximate=True)

def _silu(x):
    return jax.nn.silu(x)

def _sigmoid(x):
    return jax.nn.sigmoid(x)

def _layernorm(x, axis=-1, eps=1e-05):
    m = jnp.mean(x, axis=axis, keepdims=True)
    v = jnp.var(x, axis=axis, keepdims=True)
    return (x - m) / jnp.sqrt(v + eps)

def _scatter_add(tgt, idx, src, axis=0):
    return tgt.at[idx].add(src)

def _segment_sum(src, seg, n):
    return jax.ops.segment_sum(src, seg, n)
kernel_name = 'mk_decoder_preln_d1_seqx_r2_cf2df2'

def setup_inputs(seed: int=0):
    np.random.seed(seed)
    _w = jnp.asarray

    def _rec_inputs():
        import jax
        import jax.numpy as jnp
        _rk = jax.random.key(seed)
        x = 7.22e-05 + 1 * jax.random.normal(jax.random.fold_in(_rk, 1), (8, 100, 512), jnp.float32)
        _lenS = 100 - jax.random.randint(jax.random.fold_in(_rk, 7), (8,), 0, max(1, 100 // 4) + 1, jnp.int32)
        _lenS2 = 722 - jax.random.randint(jax.random.fold_in(_rk, 8), (8,), 0, max(1, 722 // 4) + 1, jnp.int32)
        _ctx_1024P = jax.random.normal(jax.random.fold_in(_rk, 11), (8, 16, 512), jnp.float32)
        _ctx_1024c = jax.random.dirichlet(jax.random.fold_in(_rk, 511), 0.3 * jnp.ones((16,), jnp.float32), (8, 722))
        _ctx_1024t = jnp.einsum('bsk,bkd->bsd', _ctx_1024c, _ctx_1024P)
        _ctx_1024t = _ctx_1024t * jax.lax.rsqrt(jnp.mean(jnp.square(_ctx_1024t)) + 1e-12) * 0.953939
        ctx_1024 = 4.13588e-05 + 0.999923 * (_ctx_1024t + 0.3 * jax.random.normal(jax.random.fold_in(_rk, 611), (8, 722, 512), jnp.float32))
        return (x, ctx_1024)
    x, ctx_1024 = _rec_inputs()

    def _L0_attn_setup():
        import jax, jax.numpy as jnp
        import numpy as np
        B, T, E, H = (1, 1024, 512, 16)
        HD = E // H
        key = jax.random.key(seed)
        ks = jax.random.split(key, 8)
        s = 0.02
        mk = lambda k, sh: jax.random.normal(k, sh, jnp.float32) * s
        return {'x': jax.random.normal(ks[0], (B, T, E), jnp.float32), 'wq': mk(ks[1], (E, E)), 'bq': jnp.zeros((E,), jnp.float32), 'wk': mk(ks[2], (E, E)), 'bk': jnp.zeros((E,), jnp.float32), 'wv': mk(ks[3], (E, E)), 'bv': jnp.zeros((E,), jnp.float32), 'wg': mk(ks[4], (E, E)), 'bg': jnp.zeros((E,), jnp.float32), 'wo': mk(ks[5], (E, E)), 'bo': jnp.zeros((E,), jnp.float32), 'wd': mk(ks[6], (H, E)), 'bd': jnp.zeros((H,), jnp.float32), 'gamma': jnp.ones((E,), jnp.float32), 'beta': jnp.zeros((E,), jnp.float32)}
    _L0_attn_all = _L0_attn_setup()
    _L0_attn_in = {k: v for k, v in _L0_attn_all.items() if k in ('wq', 'bq', 'wk', 'bk', 'wv', 'bv', 'wg', 'bg', 'wo', 'bo', 'wd', 'bd', 'gamma', 'beta')}
    del _L0_attn_all

    def _L0_xattn_setup():
        import jax, jax.numpy as jnp
        import numpy as np
        DIM = 512
        HEADS = 16
        HEAD_DIM = DIM // HEADS
        key = jax.random.key(seed)
        ks = jax.random.split(key, 11)
        B, Sq, Skv = (4, 1024, 1024)
        s = 1.0 / np.sqrt(DIM)
        return {'query': jax.random.normal(ks[0], (B, Sq, DIM), jnp.float32), 'key': jax.random.normal(ks[1], (B, Skv, DIM), jnp.float32), 'value': jax.random.normal(ks[2], (B, Skv, DIM), jnp.float32), 'Wq': jax.random.normal(ks[3], (DIM, DIM), jnp.float32) * s, 'bq': jnp.zeros((DIM,), jnp.float32), 'Wk': jax.random.normal(ks[4], (DIM, DIM), jnp.float32) * s, 'bk': jnp.zeros((DIM,), jnp.float32), 'Wv': jax.random.normal(ks[5], (DIM, DIM), jnp.float32) * s, 'bv': jnp.zeros((DIM,), jnp.float32), 'Wo': jax.random.normal(ks[6], (DIM, DIM), jnp.float32) * s, 'bo': jnp.zeros((DIM,), jnp.float32)}
    _L0_xattn_all = _L0_xattn_setup()
    _L0_xattn_in = {k: v for k, v in _L0_xattn_all.items() if k in ('Wq', 'bq', 'Wk', 'bk', 'Wv', 'bv', 'Wo', 'bo')}
    del _L0_xattn_all

    def _L0_ffn_setup():
        import jax, jax.numpy as jnp
        import numpy as np
        B, T, D, H, R, N = (16, 512, 512, 128, 64, 8)
        key = jax.random.key(seed)
        ks = jax.random.split(key, 8)
        s = lambda k, shape, fan: jax.random.normal(k, shape, jnp.float32) / np.sqrt(fan)
        return {'x': jax.random.normal(ks[0], (B, T, D), jnp.float32), 'W_base': s(ks[1], (D, D), D), 'b_base': jnp.zeros((D,), jnp.float32), 'W_enc': s(ks[2], (N, D, H), D), 'b_enc': jnp.zeros((N, H), jnp.float32), 'W_dec': s(ks[3], (N, H, D), H), 'b_dec': jnp.zeros((N, D), jnp.float32), 'W_down': s(ks[4], (N, D, R), D), 'b_down': jnp.zeros((N, R), jnp.float32), 'W_up': s(ks[5], (N, R, D), R), 'b_up': jnp.zeros((N, D), jnp.float32), 'connected_idx': jnp.arange(N, dtype=jnp.int32)}
    _L0_ffn_all = _L0_ffn_setup()
    _L0_ffn_in = {k: v for k, v in _L0_ffn_all.items() if k in ('W_base', 'b_base', 'W_enc', 'b_enc', 'W_dec', 'b_dec', 'W_down', 'b_down', 'W_up', 'b_up', 'connected_idx')}
    del _L0_ffn_all
    return {'x': x, 'ctx_1024': ctx_1024, 'L0_attn_wq': _L0_attn_in['wq'], 'L0_attn_bq': _L0_attn_in['bq'], 'L0_attn_wk': _L0_attn_in['wk'], 'L0_attn_bk': _L0_attn_in['bk'], 'L0_attn_wv': _L0_attn_in['wv'], 'L0_attn_bv': _L0_attn_in['bv'], 'L0_attn_wg': _L0_attn_in['wg'], 'L0_attn_bg': _L0_attn_in['bg'], 'L0_attn_wo': _L0_attn_in['wo'], 'L0_attn_bo': _L0_attn_in['bo'], 'L0_attn_wd': _L0_attn_in['wd'], 'L0_attn_bd': _L0_attn_in['bd'], 'L0_attn_gamma': _L0_attn_in['gamma'], 'L0_attn_beta': _L0_attn_in['beta'], 'L0_xattn_Wq': _L0_xattn_in['Wq'], 'L0_xattn_bq': _L0_xattn_in['bq'], 'L0_xattn_Wk': _L0_xattn_in['Wk'], 'L0_xattn_bk': _L0_xattn_in['bk'], 'L0_xattn_Wv': _L0_xattn_in['Wv'], 'L0_xattn_bv': _L0_xattn_in['bv'], 'L0_xattn_Wo': _L0_xattn_in['Wo'], 'L0_xattn_bo': _L0_xattn_in['bo'], 'L0_ffn_W_base': _L0_ffn_in['W_base'], 'L0_ffn_b_base': _L0_ffn_in['b_base'], 'L0_ffn_W_enc': _L0_ffn_in['W_enc'], 'L0_ffn_b_enc': _L0_ffn_in['b_enc'], 'L0_ffn_W_dec': _L0_ffn_in['W_dec'], 'L0_ffn_b_dec': _L0_ffn_in['b_dec'], 'L0_ffn_W_down': _L0_ffn_in['W_down'], 'L0_ffn_b_down': _L0_ffn_in['b_down'], 'L0_ffn_W_up': _L0_ffn_in['W_up'], 'L0_ffn_b_up': _L0_ffn_in['b_up'], 'L0_ffn_connected_idx': _L0_ffn_in['connected_idx']}

def reference(x, ctx_1024, L0_attn_wq, L0_attn_bq, L0_attn_wk, L0_attn_bk, L0_attn_wv, L0_attn_bv, L0_attn_wg, L0_attn_bg, L0_attn_wo, L0_attn_bo, L0_attn_wd, L0_attn_bd, L0_attn_gamma, L0_attn_beta, L0_xattn_Wq, L0_xattn_bq, L0_xattn_Wk, L0_xattn_bk, L0_xattn_Wv, L0_xattn_bv, L0_xattn_Wo, L0_xattn_bo, L0_ffn_W_base, L0_ffn_b_base, L0_ffn_W_enc, L0_ffn_b_enc, L0_ffn_W_dec, L0_ffn_b_dec, L0_ffn_W_down, L0_ffn_b_down, L0_ffn_W_up, L0_ffn_b_up, L0_ffn_connected_idx):
    import jax
    import jax.numpy as jnp

    def _L0_attn_ref(x, wq, bq, wk, bk, wv, bv, wg, bg, wo, bo, wd, bd, gamma, beta):
        import jax, jax.numpy as jnp
        import numpy as np
        B, T, E, H = (1, 1024, 512, 16)
        HD = E // H
        Bx, Tx, Ex = x.shape
        scale = jnp.sqrt(jnp.asarray(HD, jnp.float32))

        def proj(w, b):
            return (x @ w.T + b).reshape(Bx, Tx, H, HD).transpose(0, 2, 1, 3)
        Q, K, V = (proj(wq, bq), proj(wk, bk), proj(wv, bv))
        inv_freq = 1.0 / 10000.0 ** (jnp.arange(0, HD, 2, dtype=jnp.float32) / HD)
        freqs = jnp.arange(Tx, dtype=jnp.float32)[:, None] * inv_freq[None, :]
        emb = jnp.concatenate([freqs, freqs], axis=-1)
        cos, sin = (jnp.cos(emb), jnp.sin(emb))

        def rope(t):
            x1, x2 = (t[..., ::2], t[..., 1::2])
            t_rot = jnp.stack([-x2, x1], axis=-1).reshape(t.shape)
            return t * cos + t_rot * sin
        Q, K = (rope(Q), rope(K))
        scores = jnp.einsum('bhqd,bhkd->bhqk', Q, K) / scale
        pd = jax.nn.sigmoid(x.mean(axis=1) @ wd.T + bd)
        log_decay = jnp.log(1.0 - jnp.exp2(-5.0 - 8.0 * pd))
        idx = jnp.arange(Tx)
        pos_diff = jnp.clip(idx[None, :] - idx[:, None], 0, None).astype(jnp.float32)
        scores = scores + pos_diff[None, None] * log_decay[:, :, None, None]
        attn = jax.nn.softmax(scores, axis=-1)
        out = jnp.einsum('bhqk,bhkd->bhqd', attn, V).transpose(0, 2, 1, 3).reshape(Bx, Tx, Ex)
        og = out.reshape(Bx, Tx, H, HD)
        mu = og.mean(axis=(1, 3), keepdims=True)
        var = ((og - mu) ** 2).mean(axis=(1, 3), keepdims=True)
        on = ((og - mu) / jnp.sqrt(var + 1e-05)).reshape(Bx, Tx, Ex) * gamma + beta
        gate = jax.nn.silu(x @ wg.T + bg)
        return gate * on @ wo.T + bo

    def _L0_xattn_ref(query, key, value, Wq, bq, Wk, bk, Wv, bv, Wo, bo):
        import jax, jax.numpy as jnp
        import numpy as np
        DIM = 512
        HEADS = 16
        HEAD_DIM = DIM // HEADS
        B = query.shape[0]
        scale = HEAD_DIM ** (-0.5)
        q = (query @ Wq.T + bq).reshape(B, -1, HEADS, HEAD_DIM)
        k = (key @ Wk.T + bk).reshape(B, -1, HEADS, HEAD_DIM)
        v = (value @ Wv.T + bv).reshape(B, -1, HEADS, HEAD_DIM)
        scores = jnp.einsum('bqhd,bkhd->bhqk', q, k) * scale
        attn = jax.nn.softmax(scores, axis=-1)
        out = jnp.einsum('bhqk,bkhd->bqhd', attn, v).reshape(B, -1, DIM)
        return out @ Wo.T + bo

    def _L0_ffn_ref(x, W_base, b_base, W_enc, b_enc, W_dec, b_dec, W_down, b_down, W_up, b_up, connected_idx):
        import jax, jax.numpy as jnp
        import numpy as np
        B, T, D, H, R, N = (16, 512, 512, 128, 64, 8)
        base = jnp.einsum('btd,de->bte', x, W_base) + b_base
        h = jax.nn.relu(jnp.einsum('btd,ndh->nbth', x, W_enc) + b_enc[:, None, None, :])
        recon = jnp.einsum('nbth,nhd->nbtd', h, W_dec) + b_dec[:, None, None, :]
        losses = jnp.mean((recon - x[None]) ** 2, axis=(2, 3))
        top1 = jnp.argmin(losses, axis=0)
        adp = connected_idx[top1]
        Wd, bd = (W_down[adp], b_down[adp])
        Wu, bu = (W_up[adp], b_up[adp])
        mid = jax.nn.relu(jnp.einsum('btd,bdr->btr', x, Wd) + bd[:, None, :])
        adapter_out = jnp.einsum('btr,brd->btd', mid, Wu) + bu[:, None, :]
        return base + adapter_out
    x = x + _L0_attn_ref(_layernorm(x, axis=-1), L0_attn_wq, L0_attn_bq, L0_attn_wk, L0_attn_bk, L0_attn_wv, L0_attn_bv, L0_attn_wg, L0_attn_bg, L0_attn_wo, L0_attn_bo, L0_attn_wd, L0_attn_bd, L0_attn_gamma, L0_attn_beta)
    x = x + _L0_xattn_ref(_layernorm(x, axis=-1), ctx_1024, ctx_1024, L0_xattn_Wq, L0_xattn_bq, L0_xattn_Wk, L0_xattn_bk, L0_xattn_Wv, L0_xattn_bv, L0_xattn_Wo, L0_xattn_bo)
    x = x + _L0_ffn_ref(_layernorm(x, axis=-1), L0_ffn_W_base, L0_ffn_b_base, L0_ffn_W_enc, L0_ffn_b_enc, L0_ffn_W_dec, L0_ffn_b_dec, L0_ffn_W_down, L0_ffn_b_down, L0_ffn_W_up, L0_ffn_b_up, L0_ffn_connected_idx)
    return x

_drawn_inputs = setup_inputs


def setup_inputs(seed=0):
    import zlib

    import numpy as np

    out = dict(_drawn_inputs(seed))
    spreads = {'L0_attn_bq': (0.0, 0.8),
     'L0_attn_bk': (0.0, 0.8),
     'L0_attn_bv': (0.0, 0.1),
     'L0_attn_bg': (0.0, 0.373),
     'L0_attn_bo': (0.0, 0.1),
     'L0_attn_bd': (0.0, 0.8),
     'L0_attn_gamma': (1.0, 0.6),
     'L0_attn_beta': (0.0, 0.8),
     'L0_xattn_bq': (0.0, 0.423),
     'L0_xattn_bk': (0.0, 0.8),
     'L0_xattn_bv': (0.0, 0.1),
     'L0_xattn_bo': (0.0, 0.1),
     'L0_ffn_b_base': (0.0, 0.1),
     'L0_ffn_b_enc': (0.0, 0.1),
     'L0_ffn_b_dec': (0.0, 0.1),
     'L0_ffn_b_down': (0.0, 0.1),
     'L0_ffn_b_up': (0.0, 0.1)}
    factors = {'L0_attn_wq': 4.557, 'L0_attn_wk': 3.976, 'L0_attn_wd': 8.0}
    for name, (base, spread) in spreads.items():
        noise = np.random.default_rng([zlib.crc32(name.encode()), seed]).standard_normal(out[name].shape)
        drawn = base * np.exp(spread * noise) if base else spread * noise
        out[name] = jnp.asarray(drawn.astype(out[name].dtype))
    for name, factor in factors.items():
        out[name] = (out[name] * factor).astype(out[name].dtype)
    return out
```

```python
from contextlib import ExitStack

import numpy as np

import concourse.bass as bass
from concourse import mybir

F32 = mybir.dt.float32
F16 = mybir.dt.float16
I32 = mybir.dt.int32
ALU = mybir.AluOpType
ACT = mybir.ActivationFunctionType
AX = mybir.AxisListType

B, T, E = 8, 100, 512
H, HD = 16, 32
S = 722
P = 128
C = E // P
HPC = P // HD
NA, HID, R = 8, 128, 64
HALF = B // 2
NT = HALF * T
TOK = B * T
TOKP = TOK + P - T
KT = -(-S // P)
SP_ = KT * P
SH = S // 2
LASTK = S - (KT - 1) * P
VW = 2 * HD + 1
WS = 16.0
SC = 1.0 / (WS * WS * float(np.sqrt(HD)))
MS = 256.0
EPS = 1e-5
MAGIC = 0x5F3759DF
NCOLS = 4 * C + NA + NA * C
QPLANES = (0, 0, 1)
KPLANES = (0, 1, 0)

WEIGHTS_A = ("wq", "wk", "wv", "wg")
WEIGHTS_B = ("wo", "xWq", "xWk", "xWv", "xWo")
ROWS = ("bg", "gamma", "beta", "bo", "bv", "xbv", "xbo", "b_base")
COLS = ("bq", "bk", "xbq", "xbk")


class Chain:

    def __init__(self, eng, sem, per):
        self.eng, self.sem, self.per, self.item, self.n = eng, sem, per, 0, 0

    def start(self, item):
        self.item, self.n = item, 0

    def step(self, ins):
        self.n += 1
        assert self.n <= self.per
        ins.then_inc(self.sem, 1)
        self.eng.wait_ge(self.sem, self.item * self.per + self.n)


NEWTON = 3
RSQRT_STEPS = 2 + 4 * NEWTON


def rsqrt(dve, chain, y, t, v):
    chain.step(dve.tensor_single_scalar(t.bitcast(I32), v.bitcast(I32), 1, ALU.logical_shift_right))
    chain.step(dve.tensor_scalar(y.bitcast(I32), t.bitcast(I32), -1.0, float(MAGIC), ALU.mult, ALU.add))
    for _ in range(NEWTON):
        chain.step(dve.tensor_tensor(t, y, y, ALU.mult))
        chain.step(dve.tensor_tensor(t, t, v, ALU.mult))
        chain.step(dve.tensor_scalar(t, t, -0.5, 1.5, ALU.mult, ALU.add))
        chain.step(dve.tensor_tensor(y, y, t, ALU.mult))


def phase_a(nc, d, keep):
    with ExitStack() as ctx:
        sb = lambda name, shape, dt: ctx.enter_context(nc.sbuf_tensor("a_" + name, shape, dt))
        sem = lambda name: ctx.enter_context(nc.semaphore("a_" + name))
        ps = ctx.enter_context(nc.psum_tensor("a_ps", [P, 8, 512], F32))
        NST = 3
        stage = sb("stage", [P, NST, C, E], F32)
        x = sb("x", [T, B, E], F32)
        wa = {w: sb(w, [P, 2, C, E], F16) for w in WEIGHTS_A}
        wsplit = {**wa, **keep.wb}
        nT = sb("nT", [P, 2, C, TOKP], F16)
        ntok = sb("ntok", [T, 2, E], F32)
        bnst = sb("bnst", [T, B, 6], F32)
        mv = sb("mv", [T, B, 2], F32)
        ve = sb("ve", [T, B], F32)
        rstd = sb("rstd", [T, B], F32)
        scr = sb("scr", [T, B], F32)
        cos = sb("cos", [P, T], F32)
        sin = sb("sin", [P, T], F32)
        bgr = sb("bgr", [P, E], F32)
        qraw = sb("qraw", [P, 2, NT], F32)
        qsw = sb("qsw", [P, 2, NT], F32)
        qcos = sb("qcos", [P, 2, NT], F32)
        qrot = sb("qrot", [P, 2, NT], F32)
        qhl = sb("qhl", [P, 2, 2, NT], F16)
        vbuf = sb("vbuf", [T, 2, H, VW], F16)
        gpre = sb("gpre", [T, 2, E], F32)
        gth = sb("gth", [T, 2, E], F32)
        gout = sb("gout", [T, 2, E], F32)
        nmean = sb("nmean", [P, C, B], F32)
        wdT = sb("wdT", [P, C, H], F32)
        bd = sb("bd", [H, 1], F32)
        dec = sb("dec", [H, 4, B], F32)
        decx = sb("decx", [H, B, H], F32)
        ones = sb("ones", [H, P], F32)

        s_x = sem("x_in")
        s_w = [sem(f"stage_in{i}") for i in range(NST)]
        s_const = sem("const_in")
        s_whi = sem("weights_hi")
        s_wlo = sem("weights_lo")
        s_init = sem("init")
        s_bn = sem("bn_stats")
        s_mv = sem("bn_aggr")
        s_rs = sem("rstd_chain")
        s_ntok = sem("normed")
        s_tp = sem("transposed")
        s_nhi = sem("nT_hi")
        s_nlo = sem("nT_lo")
        s_qk = sem("qk_product")
        s_raw = sem("qk_raw")
        s_sw = sem("qk_swapped")
        s_sn = sem("qk_sin")
        s_cs = sem("qk_cos")
        s_rot = sem("qk_rotated")
        s_qhi = sem("qk_hi")
        s_qlo = sem("qk_lo")
        s_qout = [sem(f"qk_stored{i}") for i in range(2)]
        s_v = sem("v_product")
        s_vhi = sem("v_hi")
        s_vlo = sem("v_lo")
        s_vout = [sem(f"v_stored{i}") for i in range(2)]
        s_g = sem("gate_product")
        s_gpre = sem("gate_biased")
        s_gth = sem("gate_tanh")
        s_gout = sem("gate_done")
        s_gst = [sem(f"gate_stored{i}") for i in range(2)]
        s_dp = sem("decay_product")
        s_da = sem("decay_act")
        s_dv = sem("decay_vec")

        NW = len(wsplit)
        ALLW = list(wsplit)
        QK = [(w, oc, hf) for w in range(2) for oc in range(C) for hf in range(2)]
        NQ = len(QK)
        qk_dram = (d["q1"], d["k1"])
        block = ctx.enter_context(nc.Block())

        @block.sync
        def _(sp):
            sp.dma_start(x[:, :, :], d["x"].rearrange("b t f -> t b f")).then_inc(s_x, 16)
            for i, w in enumerate(ALLW):
                if i >= NST:
                    sp.wait_ge(s_wlo, i - NST + 1)
                sp.dma_start(stage[:, i % NST], d["w"][w]).then_inc(s_w[i % NST], 16)
            for u, (w, oc, hf) in enumerate(QK):
                sp.wait_ge(s_qlo, u + 1)
                for pl in range(2):
                    sp.dma_start(qk_dram[w][pl, oc * P:(oc + 1) * P, hf * NT:(hf + 1) * NT],
                                 qhl[:, u % 2, pl, :]).then_inc(s_qout[u % 2], 16)
                if u % 2:
                    b = u // 2
                    sp.wait_ge(s_vlo, b + 1)
                    sp.dma_start(d["v1"][b], vbuf[:, b % 2].rearrange("t h w -> t (h w)")).then_inc(s_vout[b % 2], 16)
                    sp.wait_ge(s_gout, b + 1)
                    sp.dma_start(d["gate"][b], gout[:, b % 2]).then_inc(s_gst[b % 2], 16)
            for i in range(2):
                sp.wait_ge(s_qout[i], 16 * NQ)
                sp.wait_ge(s_vout[i], 8 * B)
                sp.wait_ge(s_gst[i], 8 * B)

        @block.gpsimd
        def _(pool):
            for dst, src in ((keep.ident[:, :], d["ident"]), (cos[:, :], d["cos"]), (sin[:, :], d["sin"]),
                             (keep.pd[:, :], d["pos_diff"]), (keep.cols[:, :], d["cols"]),
                             (wdT[:, :, :], d["wd"]), (bd[:, :], d["bd"]), (bgr[:, :], d["rows"][0:1, :].broadcast_to((P, E)))):
                pool.dma_start(dst, src).then_inc(s_const, 16)
            pool.memset(nT[:, :, :, TOK:TOKP], 0.0).then_inc(s_init, 1)
            pool.memset(vbuf[:, :, :, HD:HD + 1], WS).then_inc(s_init, 1)
            pool.memset(ones[:, :], 1.0).then_inc(s_init, 1)
            pool.wait_ge(s_const, 16 * 8)
            for u in range(NQ):
                pool.wait_ge(s_raw, u + 1)
                if u >= 2:
                    pool.wait_ge(s_rot, u - 1)
                pool.tensor_tensor(qcos[:, u % 2].rearrange("p (b t) -> p b t", t=T),
                                   qraw[:, u % 2].rearrange("p (b t) -> p b t", t=T),
                                   cos[:, None, :].broadcast_to((P, HALF, T)), ALU.mult).then_inc(s_cs, 1)
                if u >= 1:
                    pool.wait_ge(s_qhi, u)
                    pool.tensor_tensor(qhl[:, (u - 1) % 2, 1], qrot[:, (u - 1) % 2], qhl[:, (u - 1) % 2, 0],
                                       ALU.subtract).then_inc(s_qlo, 1)
            pool.wait_ge(s_qhi, NQ)
            pool.tensor_tensor(qhl[:, (NQ - 1) % 2, 1], qrot[:, (NQ - 1) % 2], qhl[:, (NQ - 1) % 2, 0],
                               ALU.subtract).then_inc(s_qlo, 1)

        @block.scalar
        def _(act):
            def weight_hi(i):
                act.wait_ge(s_w[i % NST], 16 * (i // NST + 1))
                act.activation(wsplit[ALLW[i]][:, 0], stage[:, i % NST], ACT.Copy, scale=WS).then_inc(s_whi, 1)

            for i in range(NST):
                weight_hi(i)
            for b in range(B):
                act.wait_ge(s_tp, b + 1)
                act.activation(nT[:, 0, :, b * T:(b + 1) * T],
                               ps[:, b % 2, 0:C * T].rearrange("p (c t) -> p c t", t=T), ACT.Copy).then_inc(s_nhi, 1)
                if NST + b < NW:
                    weight_hi(NST + b)
            act.wait_ge(s_const, 16 * 8)
            act.wait_ge(s_dv, 1)

            def raw(u):
                w, oc, hf = QK[u]
                act.wait_ge(s_qk, u + 1)
                if u >= 2:
                    act.wait_ge(s_cs, u - 1)
                    act.wait_ge(s_sw, u - 1)
                act.activation(qraw[:, u % 2], ps[:, 2 + u % 2, 0:NT], ACT.Identity,
                               bias=keep.cols[:, w * C + oc:w * C + oc + 1]).then_inc(s_raw, 1)

            def hi(u):
                act.wait_ge(s_rot, u + 1)
                if u >= 2:
                    act.wait_ge(s_qout[u % 2], 32 * (u // 2))
                act.activation(qhl[:, u % 2, 0], qrot[:, u % 2], ACT.Copy).then_inc(s_qhi, 1)

            def vg(b):
                act.wait_ge(s_v, b + 1)
                if b >= 2:
                    act.wait_ge(s_vout[b % 2], 16 * (b // 2))
                act.wait_ge(s_init, 3)
                act.activation(vbuf[:, b % 2, :, 0:HD], ps[0:T, 4 + b % 2, :].rearrange("t (h w) -> t h w", w=HD),
                               ACT.Copy).then_inc(s_vhi, 1)
                act.wait_ge(s_gpre, b + 1)
                if b >= 2:
                    act.wait_ge(s_gout, b - 1)
                act.activation(gth[:, b % 2], gpre[:, b % 2], ACT.Tanh, scale=0.5).then_inc(s_gth, 1)

            for u in range(NQ):
                raw(u)
                if u >= 1:
                    hi(u - 1)
                if u % 2:
                    vg(u // 2)
            hi(NQ - 1)
            act.wait_ge(s_dp, 1)
            act.wait_ge(s_dv, 2)
            act.activation(dec[:, 1], dec[:, 0], ACT.Exp, scale=-1.0).then_inc(s_da, 1)
            act.wait_ge(s_dv, 4)
            act.activation(dec[:, 3], dec[:, 2], ACT.Exp, scale=-8.0 * float(np.log(2.0)),
                           bias=0.0).then_inc(s_da, 1)
            act.wait_ge(s_dv, 5)
            act.activation(dec[:, 1], dec[:, 0], ACT.Ln).then_inc(s_da, 1)

        def lo_and_mean(dve, b):
            src = ps[:, b % 2, 0:C * T].rearrange("p (c t) -> p c t", t=T)
            dve.wait_ge(s_nhi, b + 1)
            dve.tensor_reduce(nmean[:, :, b], src, AX.X, ALU.add)
            dve.tensor_tensor(nT[:, 1, :, b * T:(b + 1) * T], src, nT[:, 0, :, b * T:(b + 1) * T],
                              ALU.subtract).then_inc(s_nlo, 1)

        @block.vector
        def _(dve):
            chain = Chain(dve, s_rs, 1 + RSQRT_STEPS)

            def weight_lo(i):
                dve.wait_ge(s_whi, i + 1)
                w = wsplit[ALLW[i]]
                dve.scalar_tensor_tensor(out=w[:, 1], in0=stage[:, i % NST], scalar=WS, in1=w[:, 0],
                                         op0=ALU.mult, op1=ALU.subtract).then_inc(s_wlo, 1)

            dve.wait_ge(s_x, 16)
            for b in range(B):
                dve.bn_stats(bnst[:, b], x[:, b]).then_inc(s_bn, 1)
            for b in range(B):
                dve.wait_ge(s_bn, b + 1)
                dve.bn_aggr(mv[:, b], bnst[:, b]).then_inc(s_mv, 1)
            dve.wait_ge(s_mv, B)
            chain.start(0)
            chain.step(dve.tensor_scalar(ve[:, :], mv[:, :, 1], EPS, None, ALU.add))
            rsqrt(dve, chain, rstd[:, :], scr[:, :], ve[:, :])
            weight_lo(0)
            for b in range(B):
                if b >= 2:
                    dve.wait_ge(s_tp, b - 1)
                dve.tensor_scalar(ntok[:, b % 2], x[:, b], mv[:, b, 0:1], rstd[:, b:b + 1],
                                  ALU.subtract, ALU.mult).then_inc(s_ntok, 1)
                if b >= 1:
                    lo_and_mean(dve, b - 1)
                if b + 1 < NW:
                    weight_lo(b + 1)
            lo_and_mean(dve, B - 1)
            dve.wait_ge(s_const, 16 * 8)
            dve.tensor_scalar(keep.cols[:, :], keep.cols[:, :], WS, None, ALU.mult).then_inc(s_dv, 1)

            def rotate(u):
                dve.wait_ge(s_raw, u + 1)
                dve.stream_shuffle(qsw[:, u % 2], qraw[:, u % 2], [i ^ 1 for i in range(32)]).then_inc(s_sw, 1)
                dve.wait_ge(s_sw, u + 1)
                v = qsw[:, u % 2].rearrange("p (b t) -> p b t", t=T)
                dve.tensor_tensor(v, v, sin[:, None, :].broadcast_to((P, HALF, T)), ALU.mult).then_inc(s_sn, 1)
                dve.wait_ge(s_sn, u + 1)
                dve.wait_ge(s_cs, u + 1)
                if u >= 2:
                    dve.wait_ge(s_qlo, u - 1)
                dve.tensor_tensor(qrot[:, u % 2], qsw[:, u % 2], qcos[:, u % 2], ALU.add).then_inc(s_rot, 1)

            def vg(b):
                dve.wait_ge(s_vhi, b + 1)
                dve.tensor_tensor(vbuf[:, b % 2, :, HD + 1:VW], ps[0:T, 4 + b % 2, :].rearrange("t (h w) -> t h w", w=HD),
                                  vbuf[:, b % 2, :, 0:HD], ALU.subtract).then_inc(s_vlo, 1)
                dve.wait_ge(s_g, b + 1)
                if b >= 2:
                    dve.wait_ge(s_gout, b - 1)
                dve.scalar_tensor_tensor(out=gpre[:, b % 2], in0=ps[0:T, 6 + b % 2, :], scalar=1.0 / WS,
                                         in1=bgr[0:T], op0=ALU.mult, op1=ALU.add).then_inc(s_gpre, 1)

            def gate(b):
                dve.wait_ge(s_gth, b + 1)
                if b >= 2:
                    dve.wait_ge(s_gst[b % 2], 16 * (b // 2))
                dve.scalar_tensor_tensor(out=gout[:, b % 2], in0=gth[:, b % 2], scalar=1.0, in1=gpre[:, b % 2],
                                         op0=ALU.add, op1=ALU.mult).then_inc(s_gout, 1)

            for u in range(NQ):
                if u % 2:
                    vg(u // 2)
                rotate(u)
                if u % 2:
                    gate(u // 2)
            dve.wait_ge(s_dp, 1)
            dve.tensor_scalar(dec[:, 0], ps[0:H, 0, 0:B], 1.0 / T, bd[:, 0:1], ALU.mult, ALU.add).then_inc(s_dv, 1)
            dve.wait_ge(s_da, 1)
            dve.tensor_scalar(dec[:, 1], dec[:, 1], 1.0, None, ALU.add).then_inc(s_dv, 1)
            dve.wait_ge(s_dv, 3)
            dve.reciprocal(dec[:, 2], dec[:, 1]).then_inc(s_dv, 1)
            dve.wait_ge(s_da, 2)
            dve.tensor_scalar(dec[:, 0], dec[:, 3], -1.0 / 32.0, 1.0, ALU.mult, ALU.add).then_inc(s_dv, 1)
            dve.wait_ge(s_da, 3)
            dve.tensor_scalar(dec[:, 2], dec[:, 1], 1.0 / SC, None, ALU.mult).then_inc(s_dv, 1)
            dve.wait_ge(s_dv, 6)
            dve.tensor_tensor(decx[:, :, :], keep.ident[0:H, None, 0:H].broadcast_to((H, B, H)),
                              dec[:, 2, :, None].broadcast_to((H, B, H)), ALU.mult).then_inc(s_dv, 1)
            dve.wait_ge(s_dp, 2)
            dve.tensor_copy(keep.ld[:, :], ps[0:T, 1, 0:B * H]).then_inc(s_dv, 1)

        @block.tensor
        def _(pe):
            pe.wait_ge(s_const, 16 * 8)
            for b in range(B):
                pe.wait_ge(s_ntok, b + 1)
                if b >= 2:
                    pe.wait_ge(s_nlo, b - 1)
                for c in range(C):
                    mm = pe.transpose(ps[:, b % 2, c * T:(c + 1) * T], ntok[:, b % 2, c * P:(c + 1) * P],
                                      keep.ident[0:T, 0:T])
                mm.then_inc(s_tp, 1)

            pe.wait_ge(s_init, 3)

            def qk(u):
                w, oc, hf = QK[u]
                if u >= 2:
                    pe.wait_ge(s_raw, u - 1)
                wt = wa[("wq", "wk")[w]]
                pe.wait_ge(s_wlo, w + 1)
                pe.wait_ge(s_nlo, HALF * (hf + 1))
                passes(pe, ps[:, 2 + u % 2, 0:NT], lambda pl, c: wt[:, pl, c, oc * P:(oc + 1) * P],
                       lambda pl, c: nT[:, pl, c, hf * NT:(hf + 1) * NT]).then_inc(s_qk, 1)

            def vg(b):
                pe.wait_ge(s_wlo, 4)
                pe.wait_ge(s_nlo, B)
                window = lambda pl, c: nT[:, pl, c, b * T:b * T + P]
                if b >= 2:
                    pe.wait_ge(s_vlo, b - 1)
                passes(pe, ps[:, 4 + b % 2, :], window, lambda pl, c: wa["wv"][:, pl, c, :]).then_inc(s_v, 1)
                if b >= 2:
                    pe.wait_ge(s_gpre, b - 1)
                passes(pe, ps[:, 6 + b % 2, :], window, lambda pl, c: wa["wg"][:, pl, c, :]).then_inc(s_g, 1)

            for u in range(NQ):
                qk(u)
                if u % 2:
                    vg(u // 2)
            for c in range(C):
                mm = pe.matmul(ps[0:H, 0, 0:B], wdT[:, c, :], nmean[:, c, :], start=(c == 0), stop=(c == C - 1))
            mm.then_inc(s_dp, 1)
            pe.wait_ge(s_dv, 7)
            pe.matmul(ps[:, 1, 0:B * H], ones[:, :], decx[:, :, :].rearrange("g b h -> g (b h)"),
                      start=True, stop=True).then_inc(s_dp, 1)


PASSES = ((0, 0), (0, 1), (1, 0))


def passes(pe, out, stationary, moving, chunks=C, start=True, stop=True):
    steps = [(c, a, b) for c in range(chunks) for a, b in PASSES]
    for i, (c, a, b) in enumerate(steps):
        mm = pe.matmul(out, stationary(a, c), moving(b, c), start=(start and i == 0),
                       stop=(stop and i == len(steps) - 1))
    return mm


class Names:
    pass


STEPS = [
    [("tnorm", 0), ("v", 0), ("sscore", 0)],
    [("v", 1), ("sscore", 1), ("c", 0)],
    [("k", 0), ("sscore", 2), ("ttrans", 0)],
    [("k", 1), ("sscore", 3), ("ssoft", 0), ("tproj", 0), ("c", 1)],
    [("k", 2)],
    [("k", 3), ("strans", 0), ("strans", 1), ("c", 2)],
    [("v", 2), ("sout", 0), ("strans", 2)],
    [("v", 3), ("sout", 1), ("strans", 3), ("c", 3)],
    [("sout", 2), ("sout", 3), ("snorm", 0)],
    [("k", 4), ("c", 4)],
    [("smean", 0), ("k", 5)],
    [("v", 4), ("c", 5)],
    [("svar", 0), ("k", 6)],
    [("k", 7), ("c", 6)],
    [("v", 5), ("sgate", 0)],
    [("c", 7)],
    [("sturn", 0)],
    [("sproj", 0)],
    [],
    [("nturn", 0)],
    [("nproj", 0)],
]
LAG_S, LAG_O = 4, 5
GROUP = HPC
NG = H // GROUP
PJ_TASKS = ("k", "v", "sscore", "strans", "sout", "smean", "svar", "sturn", "sproj", "nturn", "nproj",
            "ttrans", "tproj")
NKU, NVU, NCX = 2 * C, KT, 2 * C
KST_DMAS, QST_DMAS, QK1_DMAS = 3 * HPC, 3 * HPC, 3


def schedule(cross, nxt, nxt2, tail):
    out = []
    for s, extra in enumerate(STEPS):
        for task, arg in extra:
            if (tail if task[0] == "t" else nxt2 if task == "c" else nxt):
                out.append((task, arg))
        if cross:
            if s < H:
                out.append(("M", s))
                if s % GROUP == GROUP - 1:
                    out.append(("W", s // GROUP))
            if 0 <= s - LAG_S < H:
                out.append(("S", s - LAG_S))
            if 0 <= s - LAG_O < H:
                out.append(("O", s - LAG_O))
    return out


def places(tasks, kinds, each):
    at, n = {}, 0
    for task in tasks:
        if task[0] in kinds:
            at[task] = n
            n += each.get(task[0], 1)
    return at, n


class Iteration:

    def __init__(self, b, par, cross=True, nxt=True, nxt2=True, tail=True):
        self.b, self.par = b, par
        self.tasks = schedule(cross, nxt, nxt2, tail)
        self.n, self.npar = b + 1, (par + 1) % 2
        self.pj, self.pj_n = places(self.tasks, PJ_TASKS, {})
        self.st, self.st_n = places(self.tasks, ("W", "S"), {"S": 2})


FULL = Iteration(1, 1)
FIRST = [Iteration(-1, 1, cross=False, tail=False), Iteration(0, 0, tail=False), Iteration(1, 1)]
LOOP_FROM, LOOP_TO = 2, 6
LAST = [Iteration(6, 0, nxt2=False), Iteration(7, 1, nxt=False, nxt2=False),
        Iteration(8, 0, cross=False, nxt=False, nxt2=False)]


def before(it):
    last = [i for i in FIRST + LAST if isinstance(it.b, int) and i.b == it.b - 1]
    return list((last[0] if last else FULL).pj)


def pj_base(it):
    if isinstance(it.b, int):
        return sum(i.pj_n for i in FIRST if i.b < it.b) + FULL.pj_n * max(0, min(it.b - LOOP_FROM, LOOP_TO - LOOP_FROM)) \
            + sum(i.pj_n for i in LAST if i.b < it.b)
    return it.b * FULL.pj_n + (sum(i.pj_n for i in FIRST) - LOOP_FROM * FULL.pj_n)


def run(eng, body):
    for it in FIRST:
        body(it)
    with eng.Fori(LOOP_FROM, LOOP_TO - 1, 2) as b:
        body(Iteration(b, LOOP_FROM % 2))
        body(Iteration(b + 1, (LOOP_FROM + 1) % 2))
    for it in LAST:
        body(it)


def phase_b(nc, d, keep):
    assert FULL.pj_n % 2 == 0 and FULL.st_n % 3 == 0 and all(i.pj_n % 2 == 0 for i in FIRST + LAST)
    with ExitStack() as ctx:
        sb = lambda name, shape, dt: ctx.enter_context(nc.sbuf_tensor("b_" + name, shape, dt))
        sem = lambda name: ctx.enter_context(nc.semaphore("b_" + name))
        ps = ctx.enter_context(nc.psum_tensor("b_ps", [P, 8, 512], F32))
        PJ, ST, MX, PV = 0, 2, 5, 7
        wb = keep.wb
        ident, cols = keep.ident, keep.cols
        ident16 = sb("ident16", [T, T], F16)
        rows = {r: sb(r, [T, E], F32) for r in ("gamma", "beta", "bo", "bv", "xbv", "xbo")}
        mean_w = sb("mean_w", [T, P], F32)
        cst = sb("cst", [P, 2, SH], F32)
        ch = sb("ch", [P, 2, 2, C, S], F16)
        kring = sb("kring", [P, 2, 2, S], F16)
        kst = sb("kst", [P, H, SP_], F16)
        v2 = sb("v2", [P, 2, KT, H, VW], F16)
        qst = sb("qst", [P, 2, H, P], F16)
        mx = sb("mx", [T, H], F32)
        wrow = sb("wrow", [T, GROUP, P], F16)
        p32 = sb("p32", [P, 3, KT // 2, T], F32)
        ph = sb("ph", [P, 2, KT, P], F16)
        pl = sb("pl", [P, 2, KT, P], F16)
        osb = sb("osb", [T, H, VW], F32)
        x1 = sb("x1", [T, 2, E], F32)
        q1 = sb("q1", [P, H, P], F16)
        k1 = sb("k1", [P, H, P], F16)
        v1 = sb("v1", [T, H, VW], F16)
        gate = sb("gate", [T, E], F32)
        xr = sb("xr", [T, E], F32)
        sc = sb("sc", [T, H, T], F32)
        mx1 = sb("mx1", [T, H], F32)
        sph = sb("sph", [T, 2, GROUP, P], F16)
        spl = sb("spl", [T, 2, GROUP, P], F16)
        sraw = sb("sraw", [T, H, VW], F32)
        og = sb("og", [T, H, HD], F32)
        tmp = sb("tmp", [T, H, HD], F32)
        small = sb("small", [T, 6, H], F32)
        bn = sb("bn", [T, 6], F32)
        mv = sb("mv", [T, 2], F32)
        ln = sb("ln", [T, 3], F32)
        turned = sb("turned", [P, 2, C, P], F16)
        q2 = sb("q2", [P, 2, C, T], F16)
        o2 = sb("o2", [T, H, HD], F32)
        rec2 = sb("rec2", [T, H], F32)
        oturned = sb("oturned", [P, 2, C, P], F16)
        x2 = sb("x2", [T, E], F32)

        s_const, s_init, s_initd = sem("rows_in"), sem("init"), sem("init_dve")
        s_cst = [sem(f"context_in{i}") for i in range(2)]
        s_chi, s_clo = sem("context_hi"), sem("context_lo")
        pj_ready = sem("projection_ready")
        s_khi, s_klo = sem("keys_hi"), sem("keys_lo")
        s_kst = [sem(f"key_stack_in{c}") for c in range(C)]
        s_vhi, s_vlo = sem("values_hi"), sem("values_lo")
        s_qst = sem("query_stack_in")
        mx_ready, mx_done, w_ready = sem("max_scores"), sem("maxima"), sem("maxima_spread")
        st_ready, st_free = sem("scores_ready"), sem("scores_used")
        s_p32, s_pl = sem("probs"), sem("probs_lo")
        pv_done, pv_free = sem("output_done"), sem("output_bank_free")
        s_tch, s_thi, s_tlo = sem("tail_chain"), sem("tail_hi"), sem("tail_lo")
        s_x1b = sem("x1_with_bias")
        s_x2, s_x2out = sem("x2"), sem("x2_stored")
        s_self = [sem(n) for n in ("self_q_in", "self_k_in", "self_v_in", "self_gate_in", "self_x_in")]
        s_bias, s_smax, s_ssub, s_sexp = sem("self_biased"), sem("self_max"), sem("self_shifted"), sem("self_probs")
        s_shi, s_slo, s_sout = sem("self_probs_hi"), sem("self_probs_lo"), sem("self_output")
        s_nch, s_mch = sem("self_norm_chain"), sem("self_group_norm_chain")
        s_scaled, s_affine, s_gated = sem("self_scaled"), sem("self_affine"), sem("self_gated")
        s_gam = sem("self_times_gamma")
        s_xb = sem("x_with_bias")
        s_ghi, s_glo = sem("self_turned_hi"), sem("self_turned_lo")
        s_x1, s_lch, s_n2 = sem("x1"), sem("ln2_chain"), sem("ln2")
        s_nhi, s_nlo, s_q2hi, s_q2lo = sem("ln2_turned_hi"), sem("ln2_turned_lo"), sem("query_hi"), sem("query_lo")
        NORM_STEPS, GROUP_STEPS, LN_STEPS, TAIL_STEPS = 5, 5 + RSQRT_STEPS, 3 + RSQRT_STEPS, 4
        block = ctx.enter_context(nc.Block())

        def after(eng, s, value, least=1):
            if not isinstance(value, int) or value >= least:
                eng.wait_ge(s, value)

        def key_stack(queue, it, c):
            queue.wait_ge(s_klo, NKU * it.n + 2 * c + 2)
            for g in range(3):
                for r in range(HPC):
                    queue.dma_start(kst[HD * g:HD * (g + 1), HPC * c + r, 0:S],
                                    kring[HD * r:HD * (r + 1), c % 2, KPLANES[g], :]).then_inc(s_kst[c], 16)

        @block.sync
        def _(sp):
            for name, r in (("gamma", 1), ("beta", 2), ("bo", 3), ("bv", 4), ("xbv", 5), ("xbo", 6)):
                sp.dma_start(rows[name][:, :], d["rows"][r:r + 1, :].broadcast_to((T, E))).then_inc(s_const, 16)
            sp.wait_ge(s_init, 1)

            def context(m, piece):
                c, hf = piece // 2, piece % 2
                after(sp, s_clo, NCX * m + piece - 1)
                sp.dma_start(cst[:, hf], d["ctx"][m, c, :, hf * SH:(hf + 1) * SH]).then_inc(s_cst[hf], 16)

            def self_inputs(n):
                after(sp, pj_ready, self_inputs.scored)
                for g in range(3):
                    for stack, src, planes, s in ((q1, d["q1"], QPLANES, s_self[0]), (k1, d["k1"], KPLANES, s_self[1])):
                        sp.dma_start(stack[HD * g:HD * (g + 1), :, 0:T],
                                     src[planes[g], :, bass.ds(n * T, T)].rearrange("(h w) t -> w h t", w=HD)).then_inc(s, 16)
                after(sp, s_sout, NG * n)
                sp.dma_start(v1[:, :, :], d["v1"][n].rearrange("t (h w) -> t h w", w=VW)).then_inc(s_self[2], 16)
                after(sp, s_gated, n)
                sp.dma_start(gate[:, :], d["gate"][n]).then_inc(s_self[3], 16)
                after(sp, s_x1, n)
                sp.dma_start(xr[:, :], d["x"][n]).then_inc(s_self[4], 16)

            for piece in range(NCX):
                context(0, piece)

            def body(it):
                for task, arg in it.tasks:
                    if task == "sscore" and arg == 0:
                        if isinstance(it.b, int) and it.b == -1:
                            self_inputs.scored = 0
                            self_inputs(0)
                    elif task == "c":
                        context(it.b + 2, arg)
                    elif task == "k" and arg % 2 and it.b is not None and ("S", 0) not in it.st:
                        key_stack(sp, it, arg // 2)
                    elif task == "tproj":
                        sp.wait_ge(s_x2, it.b)
                        sp.dma_start(d["x2"][it.b - 1], x2[:, :]).then_inc(s_x2out, 16)
                    elif task == "nproj":
                        sp.wait_ge(s_q2lo, C * it.n + C)
                        for g in range(3):
                            for r in range(HPC):
                                sp.dma_start(qst[HD * g:HD * (g + 1), it.npar, r:H:HPC, 0:T],
                                             q2[HD * r:HD * (r + 1), QPLANES[g], :, :]).then_inc(s_qst, 16)
                        if ("c", 0) in it.tasks:
                            self_inputs.scored = pj_base(it) + it.pj[("sscore", NG - 1)] + 1
                            self_inputs(it.b + 2)

            run(sp, body)
            sp.wait_ge(s_x2out, 16 * B)

        @block.gpsimd
        def _(pool):
            pool.memset(kst[:, :, :].bitcast(F32), 0.0).then_inc(s_init, 1)
            pool.wait_ge(s_init, 1)
            pool.memset(kst[96:97, :, 0:S], MS).then_inc(s_init, 1)
            pool.wait_ge(s_init, 2)
            pool.memset(qst[:, :, :, :].bitcast(F32), 0.0).then_inc(s_init, 1)
            pool.memset(v2[:, :, :, :, HD:HD + 1], WS).then_inc(s_init, 1)
            pool.wait_ge(s_const, 16 * 6)

            def split(m, piece, par):
                c, hf = piece // 2, piece % 2
                dst = ch[:, par, :, c, hf * SH:(hf + 1) * SH]
                pool.wait_ge(s_chi, NCX * m + piece + 1)
                pool.tensor_tensor(dst[:, 1], cst[:, hf], dst[:, 0], ALU.subtract).then_inc(s_clo, 1)

            for piece in range(NCX):
                split(0, piece, 0)

            def body(it):
                st_base, n = FULL.st_n * it.b, it.n
                for task, arg in it.tasks:
                    if task == "c":
                        split(it.b + 2, arg, it.par)
                    elif task == "S":
                        for t in range(2):
                            pool.wait_ge(st_free, st_base + it.st[("S", arg)] + t + 1)
                            half = slice(t * KT // 2, (t + 1) * KT // 2)
                            pool.tensor_tensor(pl[:, arg % 2, half, 0:T], p32[:, (2 * arg + t) % 3],
                                               ph[:, arg % 2, half, 0:T], ALU.subtract).then_inc(s_pl, 1)
                    elif task == "ssoft":
                        pool.wait_ge(s_self[4], 16 * (n + 1))
                        pool.tensor_tensor(xr[:, :], xr[:, :], rows["bo"][:, :], ALU.add).then_inc(s_xb, 1)
                    elif task == "svar":
                        pool.wait_ge(s_scaled, n + 1)
                        flat = og[:, :, :].rearrange("t h w -> t (h w)")
                        pool.tensor_tensor(flat, flat, rows["gamma"][:, :], ALU.mult).then_inc(s_gam, 1)
                        pool.wait_ge(s_gam, n + 1)
                        pool.tensor_tensor(flat, flat, rows["beta"][:, :], ALU.add).then_inc(s_affine, 1)
                    elif task == "nturn":
                        pool.wait_ge(s_n2, n + 1)
                        pool.tensor_tensor(x1[:, it.npar], x1[:, it.npar], rows["xbo"][:, :], ALU.add).then_inc(s_x1b, 1)

            run(pool, body)

        @block.scalar
        def _(act):
            act.wait_ge(s_init, 4)
            act.wait_ge(s_initd, 5)

            def context_hi(m, piece, par):
                c, hf = piece // 2, piece % 2
                act.wait_ge(s_cst[hf], 16 * (C * m + c + 1))
                act.activation(ch[:, par, 0, c, hf * SH:(hf + 1) * SH], cst[:, hf], ACT.Copy).then_inc(s_chi, 1)

            for piece in range(NCX):
                context_hi(0, piece, 0)

            def body(it):
                base, st_base, b, n = pj_base(it), FULL.st_n * it.b, it.b, it.n
                for task, arg in it.tasks:
                    if task == "c":
                        if arg == 0:
                            after(act, s_vlo, NVU * n)
                            after(act, s_klo, NKU * n)
                        context_hi(b + 2, arg, it.par)
                        continue
                    bank = PJ + it.pj.get((task, arg), 0) % 2
                    ready = base + it.pj.get((task, arg), 0) + 1
                    if task == "k":
                        oc, hf = arg // 2, arg % 2
                        act.wait_ge(pj_ready, ready)
                        if hf == 0:
                            if oc >= 2:
                                act.wait_ge(s_kst[oc - 2], 16 * KST_DMAS * (n + 1))
                            else:
                                after(act, s_kst[oc + 2], 16 * KST_DMAS * n)
                        act.activation(kring[:, oc % 2, 0, hf * SH:(hf + 1) * SH], ps[:, bank, 0:SH], ACT.Identity,
                                       bias=cols[:, 3 * C + oc:3 * C + oc + 1]).then_inc(s_khi, 1)
                    elif task == "v":
                        act.wait_ge(pj_ready, ready)
                        if arg == 0:
                            after(act, pv_done, H * b)
                        m = P if arg < KT - 1 else LASTK
                        act.activation(v2[0:m, it.npar, arg, :, 0:HD], ps[0:m, bank, :].rearrange("p (h w) -> p h w", w=HD),
                                       ACT.Copy).then_inc(s_vhi, 1)
                    elif task == "W":
                        act.wait_ge(st_ready, st_base + it.st[(task, arg)] + 1)
                        act.activation(qst[96:97, it.par, GROUP * arg:GROUP * (arg + 1), 0:T],
                                       ps[96:97, ST + it.st[(task, arg)] % 3, 0:GROUP * T].rearrange("p (h t) -> p h t", t=T),
                                       ACT.Copy).then_inc(st_free, 1)
                    elif task == "S":
                        for t in range(2):
                            use = it.st[(task, arg)] + t
                            src = ps[:, ST + use % 3, 0:KT // 2 * T].rearrange("p (k t) -> p k t", t=T)
                            act.wait_ge(st_ready, st_base + use + 1)
                            after(act, s_pl, 2 * H * b + 2 * arg + t - 2)
                            act.activation(p32[:, (2 * arg + t) % 3], src, ACT.Exp, scale=SC).then_inc(s_p32, 1)
                            if t == 0:
                                after(act, pv_done, H * b + arg - 1)
                            act.activation(ph[:, arg % 2, t * KT // 2:(t + 1) * KT // 2, 0:T], src, ACT.Exp,
                                           scale=SC).then_inc(st_free, 1)
                        if arg % GROUP == GROUP - 1 and ("k", 0) in it.pj:
                            key_stack(act, it, arg // GROUP)
                    elif task == "ssoft":
                        act.wait_ge(s_ssub, n + 1)
                        act.activation(sc[:, :, :], sc[:, :, :], ACT.Exp, scale=SC).then_inc(s_sexp, 1)
                    elif task == "strans":
                        act.wait_ge(pj_ready, ready)
                        if arg >= 2 or not isinstance(n, int) or n > 0:
                            act.wait_ge(s_sout, NG * n + arg - 1)
                        act.activation(sph[:, arg % 2, :, 0:T], ps[0:T, bank, 0:GROUP * T].rearrange("p (h t) -> p h t", t=T),
                                       ACT.Copy).then_inc(s_shi, 1)
                    elif task in ("sturn", "nturn", "ttrans"):
                        dst, s = {"sturn": (turned, s_ghi), "nturn": (turned, s_nhi), "ttrans": (oturned, s_thi)}[task]
                        act.wait_ge(pj_ready, ready)
                        act.activation(dst[:, 0, :, 0:T], ps[:, bank, 0:C * T].rearrange("p (c t) -> p c t", t=T),
                                       ACT.Copy).then_inc(s, 1)
                    elif task == "nproj":
                        act.wait_ge(pj_ready, ready)
                        after(act, s_qst, 16 * QST_DMAS * n)
                        for oc in range(C):
                            act.activation(q2[:, 0, oc], ps[:, bank, oc * T:(oc + 1) * T], ACT.Identity,
                                           bias=cols[:, 2 * C + oc:2 * C + oc + 1]).then_inc(s_q2hi, 1)

            run(act, body)

        @block.vector
        def _(dve):
            dve.memset(wrow[:, :, :].bitcast(F32), 0.0).then_inc(s_initd, 1)
            dve.memset(mean_w[:, :], 1.0 / (T * HD)).then_inc(s_initd, 1)
            dve.tensor_copy(ident16[:, :], ident[0:T, 0:T]).then_inc(s_initd, 1)
            dve.memset(ph[:, :, :, T:P], 0.0).then_inc(s_initd, 1)
            dve.memset(pl[:, :, :, T:P], 0.0)
            dve.memset(sph[:, :, :, T:P], 0.0)
            dve.memset(spl[:, :, :, T:P], 0.0)
            dve.memset(turned[:, :, :, T:P], 0.0)
            dve.memset(oturned[:, :, :, T:P], 0.0)
            dve.memset(q1[:, :, T:P], 0.0)
            dve.memset(k1[:, :, T:P], 0.0).then_inc(s_initd, 1)
            dve.wait_ge(s_initd, 5)
            dve.wait_ge(s_init, 4)
            dve.wait_ge(s_const, 16 * 6)
            norm, group = Chain(dve, s_nch, NORM_STEPS), Chain(dve, s_mch, GROUP_STEPS)
            lnorm, tail = Chain(dve, s_lch, LN_STEPS), Chain(dve, s_tch, TAIL_STEPS)
            ogf = og[:, :, :].rearrange("t h w -> t (h w)")
            spread = lambda v: v[:, :, None].broadcast_to((T, H, HD))

            def softmax_out(chain, raw, rec, out, bias):
                chain.step(dve.reciprocal(rec, raw[:, :, HD]))
                chain.step(dve.tensor_tensor(out, raw[:, :, 0:HD], raw[:, :, HD + 1:VW], ALU.add))
                chain.step(dve.tensor_tensor(out, out, spread(rec), ALU.mult))
                chain.step(dve.tensor_tensor(out, out, bias.rearrange("t (h w) -> t h w", w=HD), ALU.add))

            def body(it):
                base, st_base, b, n = pj_base(it), FULL.st_n * it.b, it.b, it.n
                for task, arg in it.tasks:
                    bank = PJ + it.pj.get((task, arg), 0) % 2
                    ready = base + it.pj.get((task, arg), 0) + 1
                    if task == "k":
                        oc, hf = arg // 2, arg % 2
                        cut = slice(hf * SH, (hf + 1) * SH)
                        dve.wait_ge(s_khi, NKU * n + arg + 1)
                        dve.scalar_tensor_tensor(out=kring[:, oc % 2, 1, cut], in0=ps[:, bank, 0:SH],
                                                 scalar=cols[:, 3 * C + oc:3 * C + oc + 1], in1=kring[:, oc % 2, 0, cut],
                                                 op0=ALU.add, op1=ALU.subtract).then_inc(s_klo, 1)
                    elif task == "v":
                        m = P if arg < KT - 1 else LASTK
                        dve.wait_ge(s_vhi, NVU * n + arg + 1)
                        dve.tensor_tensor(v2[0:m, it.npar, arg, :, HD + 1:VW], ps[0:m, bank, :].rearrange("p (h w) -> p h w", w=HD),
                                          v2[0:m, it.npar, arg, :, 0:HD], ALU.subtract).then_inc(s_vlo, 1)
                    elif task == "M":
                        dve.wait_ge(mx_ready, H * b + arg + 1)
                        if arg % GROUP == 0:
                            after(dve, w_ready, NG * b + arg // GROUP)
                        dve.tensor_reduce(mx[:, arg:arg + 1], ps[0:T, MX:MX + 2, 0:SH], AX.XY, ALU.max).then_inc(mx_done, 1)
                    elif task == "W":
                        dve.wait_ge(mx_done, H * b + GROUP * (arg + 1))
                        if arg >= 1:
                            dve.wait_ge(st_ready, st_base + it.st[(task, arg - 1)] + 1)
                        else:
                            after(dve, st_ready, st_base)
                        dve.tensor_scalar(wrow[:, :, 96], mx[:, GROUP * arg:GROUP * (arg + 1)], -1.0 / MS, None,
                                          ALU.mult).then_inc(w_ready, 1)
                    elif task == "O":
                        if arg % GROUP == GROUP - 1:
                            g = arg // GROUP
                            dve.wait_ge(pv_done, H * b + arg + 1)
                            if g == 0:
                                after(dve, s_tch, TAIL_STEPS * (b - 1))
                            dve.tensor_copy(osb[:, GROUP * g:GROUP * (g + 1)],
                                            ps[0:T, PV, 0:GROUP * VW].rearrange("p (h w) -> p h w", w=VW)).then_inc(pv_free, 1)
                    elif task == "tnorm":
                        dve.wait_ge(pv_free, NG * b)
                        after(dve, s_tlo, b - 1)
                        tail.start(b - 1)
                        softmax_out(tail, osb, rec2[:, :], o2[:, :, :], rows["xbv"][:, :])
                    elif task in ("sturn", "nturn", "ttrans"):
                        dst, hi, lo, k = {"sturn": (turned, s_ghi, s_glo, n + 1), "nturn": (turned, s_nhi, s_nlo, n + 1),
                                          "ttrans": (oturned, s_thi, s_tlo, b)}[task]
                        dve.wait_ge(hi, k)
                        dve.tensor_tensor(dst[:, 1, :, 0:T], ps[:, bank, 0:C * T].rearrange("p (c t) -> p c t", t=T),
                                          dst[:, 0, :, 0:T], ALU.subtract).then_inc(lo, 1)
                    elif task == "tproj":
                        dve.wait_ge(pj_ready, ready)
                        dve.wait_ge(s_x1b, b)
                        after(dve, s_x2out, 16 * (b - 1))
                        dve.scalar_tensor_tensor(out=x2[:, :], in0=ps[0:T, bank, :], scalar=1.0 / WS,
                                                 in1=x1[:, it.npar], op0=ALU.mult, op1=ALU.add).then_inc(s_x2, 1)
                    elif task == "sscore":
                        dve.wait_ge(pj_ready, ready)
                        if arg == 0:
                            after(dve, s_slo, NG * n)
                        for j in range(GROUP):
                            h = GROUP * arg + j
                            ins = dve.scalar_tensor_tensor(out=sc[:, h], in0=keep.pd[:, :], scalar=keep.ld[:, bass.ds(n * H + h, 1)],
                                                           in1=ps[0:T, bank, j * T:(j + 1) * T], op0=ALU.mult, op1=ALU.add)
                        ins.then_inc(s_bias, 1)
                    elif task == "ssoft":
                        dve.wait_ge(s_bias, NG * (n + 1))
                        dve.tensor_reduce(mx1[:, :], sc[:, :, :], AX.X, ALU.max).then_inc(s_smax, 1)
                        dve.wait_ge(s_smax, n + 1)
                        dve.tensor_tensor(sc[:, :, :], sc[:, :, :], mx1[:, :, None].broadcast_to((T, H, T)),
                                          ALU.subtract).then_inc(s_ssub, 1)
                    elif task == "strans":
                        dve.wait_ge(s_shi, NG * n + arg + 1)
                        dve.tensor_tensor(spl[:, arg % 2, :, 0:T], ps[0:T, bank, 0:GROUP * T].rearrange("p (h t) -> p h t", t=T),
                                          sph[:, arg % 2, :, 0:T], ALU.subtract).then_inc(s_slo, 1)
                    elif task == "sout":
                        dve.wait_ge(pj_ready, ready)
                        dve.tensor_copy(sraw[:, GROUP * arg:GROUP * (arg + 1)],
                                        ps[0:T, bank, 0:GROUP * VW].rearrange("p (h w) -> p h w", w=VW)).then_inc(s_sout, 1)
                    elif task == "snorm":
                        dve.wait_ge(s_sout, NG * (n + 1))
                        norm.start(n)
                        softmax_out(norm, sraw, small[:, 0], og[:, :, :], rows["bv"][:, :])
                        norm.step(dve.tensor_reduce(small[:, 1], og[:, :, :], AX.X, ALU.add))
                    elif task == "smean":
                        group.start(n)
                        dve.wait_ge(pj_ready, ready)
                        group.step(dve.tensor_copy(small[:, 2], ps[0:T, bank, 0:H]))
                        group.step(dve.tensor_tensor(og[:, :, :], og[:, :, :], spread(small[:, 2]), ALU.subtract))
                        group.step(dve.tensor_tensor(tmp[:, :, :], og[:, :, :], og[:, :, :], ALU.mult))
                        group.step(dve.tensor_reduce(small[:, 3], tmp[:, :, :], AX.X, ALU.add))
                    elif task == "svar":
                        dve.wait_ge(pj_ready, ready)
                        group.step(dve.tensor_scalar(small[:, 2], ps[0:T, bank, 0:H], EPS, None, ALU.add))
                        rsqrt(dve, group, small[:, 4], small[:, 5], small[:, 2])
                        dve.tensor_tensor(og[:, :, :], og[:, :, :], spread(small[:, 4]), ALU.mult).then_inc(s_scaled, 1)
                    elif task == "sgate":
                        dve.wait_ge(s_affine, n + 1)
                        dve.wait_ge(s_self[3], 16 * (n + 1))
                        dve.scalar_tensor_tensor(out=ogf, in0=ogf, scalar=0.5, in1=gate[:, :], op0=ALU.mult,
                                                 op1=ALU.mult).then_inc(s_gated, 1)
                    elif task == "sproj":
                        dve.wait_ge(pj_ready, ready)
                        dve.wait_ge(s_xb, n + 1)
                        after(dve, s_x2, n - 1)
                        dve.scalar_tensor_tensor(out=x1[:, it.npar], in0=ps[0:T, bank, :], scalar=1.0 / WS,
                                                 in1=xr[:, :], op0=ALU.mult, op1=ALU.add).then_inc(s_x1, 1)
                        dve.wait_ge(s_x1, n + 1)
                        lnorm.start(n)
                        lnorm.step(dve.bn_stats(bn[:, :], x1[:, it.npar]))
                        dve.memset(ln[:, 2:3], 0.0)
                        lnorm.step(dve.bn_aggr(mv[:, :], bn[:, :]))
                        lnorm.step(dve.tensor_scalar(ln[:, 0:1], mv[:, 1:2], EPS, None, ALU.add))
                        rsqrt(dve, lnorm, ln[:, 1:2], ln[:, 2:3], ln[:, 0:1])
                        dve.tensor_scalar(ogf, x1[:, it.npar], mv[:, 0:1], ln[:, 1:2], ALU.subtract,
                                          ALU.mult).then_inc(s_n2, 1)
                    elif task == "nproj":
                        for oc in range(C):
                            dve.wait_ge(s_q2hi, C * n + C)
                            ins = dve.scalar_tensor_tensor(out=q2[:, 1, oc], in0=ps[:, bank, oc * T:(oc + 1) * T],
                                                           scalar=cols[:, 2 * C + oc:2 * C + oc + 1], in1=q2[:, 0, oc],
                                                           op0=ALU.add, op1=ALU.subtract).then_inc(s_q2lo, 1)

            run(dve, body)

        def last_read(it, use):
            order = list(it.pj)
            b, n = it.b, it.n
            if use < 0:
                if isinstance(b, int) and b == FIRST[0].b:
                    return s_init, 0
                order, b, n = before(it), b - 1, n - 1
            task, arg = order[use]
            return {"k": (s_klo, NKU * n + arg + 1), "v": (s_vlo, NVU * n + arg + 1), "sscore": (s_bias, NG * n + arg + 1),
                    "strans": (s_slo, NG * n + arg + 1), "sout": (s_sout, NG * n + arg + 1),
                    "smean": (s_mch, GROUP_STEPS * n + 1), "svar": (s_mch, GROUP_STEPS * n + 5),
                    "sturn": (s_glo, n + 1), "sproj": (s_x1, n + 1), "nturn": (s_nlo, n + 1), "nproj": (s_q2lo, C * n + C),
                    "ttrans": (s_tlo, b), "tproj": (s_x2, b)}[task]

        @block.tensor
        def _(pe):
            pe.wait_ge(s_init, 4)
            pe.wait_ge(s_initd, 5)

            def body(it):
                base, st_base, b, n = pj_base(it), FULL.st_n * it.b, it.b, it.n
                for task, arg in it.tasks:
                    use = it.pj.get((task, arg))
                    if use is not None:
                        bank = PJ + use % 2
                        s, value = last_read(it, use - 2)
                        after(pe, s, value)
                    if task == "k":
                        oc, hf = arg // 2, arg % 2
                        pe.wait_ge(s_clo, NCX * (n + 1))
                        passes(pe, ps[:, bank, 0:SH], lambda p, c: wb["xWk"][:, p, c, oc * P:(oc + 1) * P],
                               lambda p, c: ch[:, it.npar, p, c, hf * SH:(hf + 1) * SH]).then_inc(pj_ready, 1)
                    elif task == "v":
                        m = P if arg < KT - 1 else LASTK
                        pe.wait_ge(s_clo, NCX * (n + 1))
                        passes(pe, ps[0:m, bank, :], lambda p, c: ch[:, it.npar, p, c, arg * P:arg * P + m],
                               lambda p, c: wb["xWv"][:, p, c, :]).then_inc(pj_ready, 1)
                    elif task == "M":
                        if arg == 0:
                            pe.wait_ge(s_qst, 16 * QST_DMAS * (b + 1))
                        if arg % HPC == 0:
                            pe.wait_ge(s_kst[arg // HPC], 16 * KST_DMAS * (b + 1))
                        after(pe, mx_done, H * b + arg)
                        for hf in range(2):
                            mm = pe.matmul(ps[:, MX + hf, 0:SH], qst[0:96, it.par, arg, :],
                                           kst[0:96, arg, hf * SH:(hf + 1) * SH], start=True, stop=True)
                        mm.then_inc(mx_ready, 1)
                    elif task == "W":
                        pe.wait_ge(w_ready, NG * b + arg + 1)
                        u = it.st[(task, arg)]
                        after(pe, st_free, st_base + u - 2)
                        for j in range(GROUP):
                            mm = pe.matmul(ps[:, ST + u % 3, j * T:(j + 1) * T], wrow[:, j, :], ident16[:, :],
                                           start=True, stop=True)
                        mm.then_inc(st_ready, 1)
                    elif task == "S":
                        pe.wait_ge(st_free, st_base + it.st[("W", arg // GROUP)] + 1)
                        for t in range(2):
                            u = it.st[(task, arg)] + t
                            after(pe, st_free, st_base + u - 2)
                            for k in range(KT // 2):
                                kt = t * KT // 2 + k
                                mm = pe.matmul(ps[:, ST + u % 3, k * T:(k + 1) * T], kst[0:97, arg, kt * P:(kt + 1) * P],
                                               qst[0:97, it.par, arg, 0:T], start=True, stop=True)
                            mm.then_inc(st_ready, 1)
                    elif task == "O":
                        if arg == 0:
                            pe.wait_ge(s_vlo, NVU * (b + 1))
                        if arg % GROUP == 0:
                            after(pe, pv_free, NG * b + arg // GROUP)
                        pe.wait_ge(s_pl, 2 * H * b + 2 * arg + 2)
                        out = ps[:, PV, (arg % GROUP) * VW:(arg % GROUP + 1) * VW]
                        for kt in range(KT):
                            m = P if kt < KT - 1 else LASTK
                            hi = lambda last: pe.matmul(out, ph[0:m, arg % 2, kt, :], v2[0:m, it.par, kt, arg, :],
                                                        start=(kt == 0), stop=last)
                            lo = lambda: pe.matmul(out[:, 0:HD + 1], pl[0:m, arg % 2, kt, :],
                                                   v2[0:m, it.par, kt, arg, 0:HD + 1], start=False, stop=False)
                            if kt < KT - 1:
                                hi(False)
                                lo()
                            else:
                                lo()
                                mm = hi(True)
                        mm.then_inc(pv_done, 1)
                    elif task == "sscore":
                        if arg == 0:
                            for s in s_self[0:2]:
                                pe.wait_ge(s, 16 * QK1_DMAS * (n + 1))
                        for j in range(GROUP):
                            h = GROUP * arg + j
                            mm = pe.matmul(ps[:, bank, j * T:(j + 1) * T], q1[0:96, h, :], k1[0:96, h, 0:T],
                                           start=True, stop=True)
                        mm.then_inc(pj_ready, 1)
                    elif task == "strans":
                        pe.wait_ge(s_sexp, n + 1)
                        for j in range(GROUP):
                            mm = pe.transpose(ps[0:T, bank, j * T:(j + 1) * T], sc[:, GROUP * arg + j, :], ident[0:T, 0:T])
                        mm.then_inc(pj_ready, 1)
                    elif task == "sout":
                        pe.wait_ge(s_slo, NG * n + arg + 1)
                        pe.wait_ge(s_self[2], 16 * (n + 1))
                        for j in range(GROUP):
                            h = GROUP * arg + j
                            out = ps[:, bank, j * VW:(j + 1) * VW]
                            pe.matmul(out, sph[:, arg % 2, j, :], v1[:, h, :], start=True, stop=False)
                            mm = pe.matmul(out[:, 0:HD + 1], spl[:, arg % 2, j, :], v1[:, h, 0:HD + 1], start=False, stop=True)
                        mm.then_inc(pj_ready, 1)
                    elif task == "smean":
                        pe.wait_ge(s_nch, NORM_STEPS * (n + 1))
                        pe.matmul(ps[:, bank, 0:H], mean_w[:, :], small[:, 1], start=True, stop=True).then_inc(pj_ready, 1)
                    elif task == "svar":
                        pe.wait_ge(s_mch, GROUP_STEPS * n + 4)
                        pe.matmul(ps[:, bank, 0:H], mean_w[:, :], small[:, 3], start=True, stop=True).then_inc(pj_ready, 1)
                    elif task in ("sturn", "nturn", "ttrans"):
                        src, s, k = {"sturn": (og, s_gated, n + 1), "nturn": (og, s_n2, n + 1), "ttrans": (o2, s_tch, TAIL_STEPS * b)}[task]
                        pe.wait_ge(s, k)
                        flat = src[:, :, :].rearrange("t h w -> t (h w)")
                        for c in range(C):
                            mm = pe.transpose(ps[:, bank, c * T:(c + 1) * T], flat[:, c * P:(c + 1) * P], ident[0:T, 0:T])
                        mm.then_inc(pj_ready, 1)
                    elif task in ("sproj", "tproj"):
                        src, w, s, k = {"sproj": (turned, "wo", s_glo, n + 1), "tproj": (oturned, "xWo", s_tlo, b)}[task]
                        pe.wait_ge(s, k)
                        passes(pe, ps[:, bank, :], lambda p, c: src[:, p, c, :], lambda p, c: wb[w][:, p, c, :]).then_inc(pj_ready, 1)
                    elif task == "nproj":
                        pe.wait_ge(s_nlo, n + 1)
                        for oc in range(C):
                            mm = passes(pe, ps[:, bank, oc * T:(oc + 1) * T], lambda p, c: wb["xWq"][:, p, c, oc * P:(oc + 1) * P],
                                        lambda p, c: turned[:, p, c, 0:T])
                        mm.then_inc(pj_ready, 1)

            run(pe, body)

WEIGHTS_C = ("base", "enc", "dec")
ADAPTER_DMAS = 4


def phase_c(nc, d, keep):
    with ExitStack() as ctx:
        sb = lambda name, shape, dt: ctx.enter_context(nc.sbuf_tensor("c_" + name, shape, dt))
        sem = lambda name: ctx.enter_context(nc.semaphore("c_" + name))
        ps = ctx.enter_context(nc.psum_tensor("c_ps", [P, 8, 512], F32))
        EN, DE, BA, MI = 0, 2, 4, 6
        stage = sb("stage", [P, 2, C, E], F32)
        base = sb("base", [P, 2, C, E], F16)
        enc = sb("enc", [P, 2, NA, C, HID], F16)
        dec = sb("dec", [HID, 2, NA, E], F16)
        x = sb("x", [T, B, E], F32)
        ntok = sb("ntok", [T, 2, E], F32)
        nT = sb("nT", [P, 2, C, TOKP], F16)
        n32 = sb("n32", [P, C, TOK], F32)
        bnst = sb("bnst", [T, B, 6], F32)
        mv = sb("mv", [T, B, 2], F32)
        ve = sb("ve", [T, 3, B], F32)
        b_enc = sb("b_enc", [P, NA], F32)
        bbase = sb("bbase", [T, E], F32)
        h32 = sb("h32", [HID, 2, NT], F32)
        hhl = sb("hhl", [HID, 2, 2, NT], F16)
        err = sb("err", [P, 2, NT], F32)
        sq = sb("sq", [P, C, NT], F32)
        sqs = sb("sqs", [P, 2, NT], F32)
        loss = sb("loss", [P, NA, B], F32)
        ones = sb("ones", [P, P], F32)
        pick = sb("pick", [1, 8, NA * B], F32)
        iota = sb("iota", [1, NA], F32)
        conn = sb("conn", [1, NA], I32)
        connf = sb("connf", [1, NA], F32)
        sel = sb("sel", [1, B], I32)
        wd32 = sb("wd32", [P, 2, C, R], F32)
        wdn = sb("wdn", [P, 2, 2, C, R], F16)
        wu32 = sb("wu32", [R, 2, E], F32)
        wup = sb("wup", [R, 2, 2, E], F16)
        bdn = sb("bdn", [R, 2, 1], F32)
        bup = sb("bup", [T, 2, E], F32)
        mid32 = sb("mid32", [R, 2, T], F32)
        mid = sb("mid", [R, 2, 2, P], F16)
        res = sb("res", [T, 2, E], F32)

        s_x = [sem(f"x2_in{b}") for b in range(B)]
        s_w = [sem(f"stage_in{i}") for i in range(2)]
        s_const, s_init = sem("const_in"), sem("init")
        s_whi, s_wlo = sem("weights_hi"), sem("weights_lo")
        s_bn, s_mv, s_rs = sem("bn_stats"), sem("bn_aggr"), sem("rstd_chain")
        s_ntok, s_tp, s_nhi, s_nlo, s_n32 = sem("normed"), sem("transposed"), sem("nT_hi"), sem("nT_lo"), sem("nT_scaled")
        s_b = sem("bias")
        s_en, s_h32, s_hhi, s_hlo = sem("encoded"), sem("hidden"), sem("hidden_hi"), sem("hidden_lo")
        s_de, s_err, s_sq, s_sum, s_loss = sem("decoded"), sem("error"), sem("squares"), sem("square_sums"), sem("losses")
        s_tot, s_pick, s_sel = sem("loss_totals"), sem("pick_chain"), sem("adapter_chosen")
        s_ad = [sem(f"adapter_in{i}") for i in range(2)]
        s_adhi, s_adlo = sem("adapter_hi"), sem("adapter_lo")
        s_ba, s_mi, s_m32, s_mhi, s_mlo = sem("base_product"), sem("middle"), sem("middle_relu"), sem("middle_hi"), sem("middle_lo")
        s_up, s_pre, s_res = sem("adapter_product"), sem("residual_with_biases"), sem("result")
        s_out = [sem(f"stored{i}") for i in range(2)]
        block = ctx.enter_context(nc.Block())

        halves = lambda t: [t[:, :, 0:NA // 2], t[:, :, NA // 2:NA]]
        src_halves = lambda t: [t[:, 0:NA // 2], t[:, NA // 2:NA]]
        LOADS = [(src_halves(d["w"]["enc"])[0], halves(enc)[0]), (src_halves(d["w"]["enc"])[1], halves(enc)[1]),
                 (src_halves(d["w"]["dec"])[0], halves(dec)[0]), (src_halves(d["w"]["dec"])[1], halves(dec)[1]),
                 (d["w"]["base"], base)]
        NL = len(LOADS)
        UNITS = [(n, hf) for n in range(NA) for hf in range(2)]
        NU = len(UNITS)

        def staged(i):
            src = LOADS[i][0]
            flat = stage[:, i % 2].rearrange("p c e -> p (c e)")
            return flat if len(src.shape) == 2 else \
                flat.rearrange("p (a b) -> p a b", b=src.shape[2]) if len(src.shape) == 3 else \
                flat.rearrange("p (a b c) -> p a b c", b=src.shape[2], c=src.shape[3])

        @block.sync
        def _(sp):
            for i in range(2):
                sp.dma_start(staged(i), LOADS[i][0]).then_inc(s_w[i], 16)
            for b in range(B):
                sp.dma_start(x[:, b], d["x2"][b]).then_inc(s_x[b], 16)
            for i in range(2, NL):
                sp.wait_ge(s_wlo, i - 1)
                sp.dma_start(staged(i), LOADS[i][0]).then_inc(s_w[i % 2], 16)
            sp.wait_ge(s_sel, 1)
            for b in range(B):
                if b >= 2:
                    sp.wait_ge(s_adlo, 2 * (b - 1))
                    sp.wait_ge(s_mhi, b - 1)
                    sp.wait_ge(s_pre, b - 1)
                a = sp.value_load(sel[0:1, b:b + 1], min_val=0, max_val=NA - 1)
                for dst, src in ((wd32[:, b % 2], d["w"]["down"]), (wu32[:, b % 2], d["w"]["up"]), (bdn[:, b % 2], d["b_down"])):
                    sp.dma_start(dst, src[a]).then_inc(s_ad[b % 2], 16)
                sp.dma_start(bup[:, b % 2], d["b_up"][bass.ds(a, 1), :].broadcast_to((T, E))).then_inc(s_ad[b % 2], 16)
                if b >= 1:
                    sp.wait_ge(s_res, b)
                    sp.dma_start(d["out"][b - 1], res[:, (b - 1) % 2]).then_inc(s_out[(b - 1) % 2], 16)
            sp.wait_ge(s_res, B)
            sp.dma_start(d["out"][B - 1], res[:, (B - 1) % 2]).then_inc(s_out[(B - 1) % 2], 16)
            for i in range(2):
                sp.wait_ge(s_out[i], 8 * B)

        @block.gpsimd
        def _(pool):
            pool.dma_start(bbase[:, :], d["rows"][7:8, :].broadcast_to((T, E))).then_inc(s_const, 16)
            pool.dma_start(conn[:, :], d["connected"]).then_inc(s_const, 16)
            pool.dma_start(iota[:, :], d["iota"]).then_inc(s_const, 16)
            pool.memset(nT[:, :, :, TOK:TOKP], 0.0).then_inc(s_init, 1)
            pool.memset(ones[:, :], 1.0).then_inc(s_init, 1)
            pool.memset(mid[:, :, :, T:P], 0.0).then_inc(s_init, 1)

            def hidden_lo(u):
                pool.wait_ge(s_hhi, u + 1)
                pool.tensor_tensor(hhl[:, u % 2, 1], h32[:, u % 2], hhl[:, u % 2, 0], ALU.subtract).then_inc(s_hlo, 1)

            def square_sums(u):
                for k in range(C - 1):
                    pool.wait_ge(s_sq, C * u + k + 2)
                    if k == 0 and u >= 2:
                        pool.wait_ge(s_loss, u - 1)
                    if k:
                        pool.wait_ge(s_sum, (C - 1) * u + k)
                    pool.tensor_tensor(sqs[:, u % 2], sqs[:, u % 2] if k else sq[:, 0], sq[:, k + 1],
                                       ALU.add).then_inc(s_sum, 1)

            for u in range(NU):
                hidden_lo(u)
                if u >= 1:
                    square_sums(u - 1)
            square_sums(NU - 1)

        @block.scalar
        def _(act):
            def weight_hi(i):
                act.wait_ge(s_w[i % 2], 16 * (i // 2 + 1))
                act.activation(LOADS[i][1][:, 0], staged(i), ACT.Copy, scale=WS).then_inc(s_whi, 1)

            weight_hi(0)
            weight_hi(1)
            for b in range(B):
                act.wait_ge(s_tp, b + 1)
                act.activation(nT[:, 0, :, b * T:(b + 1) * T],
                               ps[:, b % 2, 0:C * T].rearrange("p (c t) -> p c t", t=T), ACT.Copy).then_inc(s_nhi, 1)
                act.activation(n32[:, :, b * T:(b + 1) * T],
                               ps[:, b % 2, 0:C * T].rearrange("p (c t) -> p c t", t=T), ACT.Copy, scale=WS).then_inc(s_n32, 1)
                if b % 2 and 2 + b // 2 < NL:
                    weight_hi(2 + b // 2)
            act.wait_ge(s_b, 1)

            def hidden(u):
                n, hf = UNITS[u]
                act.wait_ge(s_en, u + 1)
                if u >= 2:
                    act.wait_ge(s_hlo, u - 1)
                    act.wait_ge(s_de, C * (u - 1))
                act.activation(h32[:, u % 2], ps[:, EN + u % 2, 0:NT], ACT.Relu, bias=b_enc[:, n:n + 1],
                               scale=1.0 / WS).then_inc(s_h32, 1)
                act.wait_ge(s_h32, u + 1)
                act.activation(hhl[:, u % 2, 0], h32[:, u % 2], ACT.Copy).then_inc(s_hhi, 1)

            def squares(u):
                for oc in range(C):
                    i = C * u + oc
                    act.wait_ge(s_err, i + 1)
                    if u >= 1:
                        act.wait_ge(s_sum, (C - 1) * u)
                    act.activation(sq[:, oc], err[:, i % 2], ACT.Square, scale=1.0 / WS).then_inc(s_sq, 1)

            for u in range(NU):
                hidden(u)
                if u >= 1:
                    squares(u - 1)
            squares(NU - 1)
            for b in range(B):
                act.wait_ge(s_ad[b % 2], 16 * ADAPTER_DMAS * (b // 2 + 1))
                if b >= 2:
                    act.wait_ge(s_up, b - 1)
                act.activation(wdn[:, b % 2, 0], wd32[:, b % 2], ACT.Copy, scale=WS).then_inc(s_adhi, 1)
                act.activation(wup[:, b % 2, 0], wu32[:, b % 2], ACT.Copy, scale=WS).then_inc(s_adhi, 1)
                act.wait_ge(s_mi, b + 1)
                act.activation(mid32[:, b % 2], ps[0:R, MI + b % 2, 0:T], ACT.Relu, bias=bdn[:, b % 2],
                               scale=1.0 / WS).then_inc(s_m32, 1)
                act.wait_ge(s_m32, b + 1)
                act.activation(mid[:, b % 2, 0, 0:T], mid32[:, b % 2], ACT.Copy).then_inc(s_mhi, 1)

        @block.vector
        def _(dve):
            chain = Chain(dve, s_rs, 1 + RSQRT_STEPS)

            def weight_lo(i):
                dve.wait_ge(s_whi, i + 1)
                dve.scalar_tensor_tensor(out=LOADS[i][1][:, 1], in0=staged(i), scalar=WS, in1=LOADS[i][1][:, 0],
                                         op0=ALU.mult, op1=ALU.subtract).then_inc(s_wlo, 1)

            for b in range(B):
                dve.wait_ge(s_x[b], 16)
                dve.bn_stats(bnst[:, b], x[:, b]).then_inc(s_bn, 1)
            for b in range(B):
                dve.wait_ge(s_bn, b + 1)
                dve.bn_aggr(mv[:, b], bnst[:, b]).then_inc(s_mv, 1)
            dve.wait_ge(s_mv, B)
            chain.start(0)
            chain.step(dve.tensor_scalar(ve[:, 0], mv[:, :, 1], EPS, None, ALU.add))
            rsqrt(dve, chain, ve[:, 1], ve[:, 2], ve[:, 0])
            dve.tensor_scalar(b_enc[:, :], keep.cols[:, 4 * C:4 * C + NA], 1.0 / WS, None, ALU.mult).then_inc(s_b, 1)

            def lo(b):
                dve.wait_ge(s_n32, b + 1)
                dve.tensor_tensor(nT[:, 1, :, b * T:(b + 1) * T], ps[:, b % 2, 0:C * T].rearrange("p (c t) -> p c t", t=T),
                                  nT[:, 0, :, b * T:(b + 1) * T], ALU.subtract).then_inc(s_nlo, 1)

            for b in range(B):
                if b >= 2:
                    dve.wait_ge(s_tp, b - 1)
                dve.tensor_scalar(ntok[:, b % 2], x[:, b], mv[:, b, 0:1], ve[:, 1, b:b + 1], ALU.subtract,
                                  ALU.mult).then_inc(s_ntok, 1)
                if b >= 1:
                    lo(b - 1)
                if b < 2:
                    weight_lo(b)
                elif b % 2:
                    weight_lo(2 + b // 2 - 1)
            lo(B - 1)
            assert NL == 5
            dve.wait_ge(s_b, 1)
            dve.wait_ge(s_const, 48)
            dve.wait_ge(s_init, 3)

            def losses(u):
                n, hf = UNITS[u]
                dve.wait_ge(s_sum, (C - 1) * (u + 1))
                dve.tensor_reduce(loss[:, n, hf * HALF:(hf + 1) * HALF], sqs[:, u % 2].rearrange("p (b t) -> p b t", t=T),
                                  AX.X, ALU.add).then_inc(s_loss, 1)

            for u in range(NU):
                n, hf = UNITS[u]
                for oc in range(C):
                    i = C * u + oc
                    dve.wait_ge(s_de, i + 1)
                    if i >= 2:
                        dve.wait_ge(s_sq, i - 1)
                    col = 4 * C + NA + n * C + oc
                    dve.scalar_tensor_tensor(out=err[:, i % 2], in0=ps[:, DE + i % 2, 0:NT], scalar=keep.cols[:, col:col + 1],
                                             in1=n32[:, oc, hf * NT:(hf + 1) * NT], op0=ALU.add,
                                             op1=ALU.subtract).then_inc(s_err, 1)
                if u >= 1:
                    losses(u - 1)
            losses(NU - 1)

            pc = Chain(dve, s_pick, 16)
            pc.start(0)
            mean, best = pick[:, 0], pick[:, 1, 0:B]
            v = lambda k: pick[:, k].rearrange("p (b n) -> p b n", n=NA)
            over_n = lambda t: t[:, :, None].broadcast_to((1, B, NA))
            over_b = lambda t: t[:, None, :].broadcast_to((1, B, NA))
            dve.wait_ge(s_tot, 1)
            pc.step(dve.tensor_scalar(mean, ps[0:1, EN, 0:NA * B], 1.0 / (T * E), None, ALU.mult))
            pc.step(dve.tensor_copy(v(2), mean.rearrange("p (n b) -> p b n", b=B)))
            pc.step(dve.tensor_reduce(best, v(2), AX.X, ALU.min))
            pc.step(dve.tensor_tensor(v(3), v(2), over_n(best), ALU.is_gt))
            pc.step(dve.tensor_scalar(v(4), v(3), float(NA), None, ALU.mult))
            pc.step(dve.tensor_tensor(v(4), v(4), over_b(iota[:, :]), ALU.add))
            pc.step(dve.tensor_reduce(best, v(4), AX.X, ALU.min))
            pc.step(dve.tensor_tensor(v(5), over_b(iota[:, :]), over_n(best), ALU.is_equal))
            pc.step(dve.tensor_copy(connf[:, :], conn[:, :]))
            pc.step(dve.tensor_tensor(v(5), v(5), over_b(connf[:, :]), ALU.mult))
            pc.step(dve.tensor_reduce(best, v(5), AX.X, ALU.add))
            neg = pick[:, 6, 0:B]
            pc.step(dve.tensor_scalar(neg, best, 0.0, float(NA), ALU.is_lt, ALU.mult))
            pc.step(dve.tensor_tensor(best, best, neg, ALU.add))
            pc.step(dve.tensor_scalar(best, best, 0.0, float(NA - 1), ALU.max, ALU.min))
            dve.tensor_copy(sel[:, :], best).then_inc(s_sel, 1)

            def finish(b):
                dve.wait_ge(s_up, b + 1)
                dve.wait_ge(s_pre, b + 1)
                if b >= 2:
                    dve.wait_ge(s_out[b % 2], 16 * (b // 2))
                dve.scalar_tensor_tensor(out=res[:, b % 2], in0=ps[0:T, BA + b % 2, :], scalar=1.0 / WS, in1=x[:, b],
                                         op0=ALU.mult, op1=ALU.add).then_inc(s_res, 1)

            for b in range(B):
                dve.tensor_tensor(x[:, b], x[:, b], bbase[:, :], ALU.add).then_inc(s_b, 1)
                dve.wait_ge(s_adhi, 2 * b + 2)
                dve.scalar_tensor_tensor(out=wdn[:, b % 2, 1], in0=wd32[:, b % 2], scalar=WS, in1=wdn[:, b % 2, 0],
                                         op0=ALU.mult, op1=ALU.subtract).then_inc(s_adlo, 1)
                dve.scalar_tensor_tensor(out=wup[:, b % 2, 1], in0=wu32[:, b % 2], scalar=WS, in1=wup[:, b % 2, 0],
                                         op0=ALU.mult, op1=ALU.subtract).then_inc(s_adlo, 1)
                dve.wait_ge(s_b, b + 2)
                dve.tensor_tensor(x[:, b], x[:, b], bup[:, b % 2], ALU.add).then_inc(s_pre, 1)
                if b >= 1:
                    finish(b - 1)
                dve.wait_ge(s_mhi, b + 1)
                dve.tensor_tensor(mid[:, b % 2, 1, 0:T], mid32[:, b % 2], mid[:, b % 2, 0, 0:T], ALU.subtract).then_inc(s_mlo, 1)
            finish(B - 1)

        @block.tensor
        def _(pe):
            for b in range(B):
                pe.wait_ge(s_ntok, b + 1)
                if b >= 2:
                    pe.wait_ge(s_nlo, b - 1)
                for c in range(C):
                    mm = pe.transpose(ps[:, b % 2, c * T:(c + 1) * T], ntok[:, b % 2, c * P:(c + 1) * P], keep.ident[0:T, 0:T])
                mm.then_inc(s_tp, 1)
            pe.wait_ge(s_init, 3)
            pe.wait_ge(s_nlo, B)

            def encode(u):
                n, hf = UNITS[u]
                pe.wait_ge(s_wlo, 1 + n // (NA // 2))
                if u >= 2:
                    pe.wait_ge(s_h32, u - 1)
                passes(pe, ps[:, EN + u % 2, 0:NT], lambda p, c: enc[:, p, n, c, :],
                       lambda p, c: nT[:, p, c, hf * NT:(hf + 1) * NT]).then_inc(s_en, 1)

            def decode(u):
                n, hf = UNITS[u]
                pe.wait_ge(s_wlo, 3 + n // (NA // 2))
                pe.wait_ge(s_hlo, u + 1)
                for oc in range(C):
                    i = C * u + oc
                    if i >= 2:
                        pe.wait_ge(s_err, i - 1)
                    passes(pe, ps[:, DE + i % 2, 0:NT], lambda p, c: dec[:, p, n, oc * P:(oc + 1) * P],
                           lambda p, c: hhl[:, u % 2, p], chunks=1).then_inc(s_de, 1)

            encode(0)
            for u in range(NU):
                if u + 1 < NU:
                    encode(u + 1)
                decode(u)
            pe.wait_ge(s_loss, NU)
            pe.matmul(ps[:, EN, 0:NA * B], ones[:, :], loss[:, :, :].rearrange("p n b -> p (n b)"),
                      start=True, stop=True).then_inc(s_tot, 1)

            def base_product(b):
                if b >= 2:
                    pe.wait_ge(s_res, b - 1)
                passes(pe, ps[:, BA + b % 2, :], lambda p, c: nT[:, p, c, b * T:b * T + P], lambda p, c: base[:, p, c, :],
                       stop=False)

            pe.wait_ge(s_wlo, NL)
            base_product(0)
            for b in range(B):
                if b + 1 < B:
                    base_product(b + 1)
                pe.wait_ge(s_adlo, 2 * b + 2)
                if b >= 2:
                    pe.wait_ge(s_mhi, b - 1)
                passes(pe, ps[0:R, MI + b % 2, 0:T], lambda p, c: wdn[:, b % 2, p, c, :],
                       lambda p, c: nT[:, p, c, b * T:(b + 1) * T]).then_inc(s_mi, 1)
                pe.wait_ge(s_mlo, b + 1)
                passes(pe, ps[:, BA + b % 2, :], lambda p, c: mid[:, b % 2, p, :], lambda p, c: wup[:, b % 2, p, :],
                       chunks=1, start=False).then_inc(s_up, 1)



def shapes_only_constants():
    inv_freq = (1.0 / 10000.0 ** (np.arange(0, HD, 2, dtype=np.float32) / np.float32(HD))).astype(np.float32)
    freqs = np.arange(T, dtype=np.float32)[:, None] * inv_freq[None, :]
    emb = np.concatenate([freqs, freqs], axis=-1)
    sign = np.where(np.arange(HD) % 2, 1.0, -1.0).astype(np.float32)
    cos = np.tile(np.cos(emb).T, (HPC, 1)).astype(np.float32)
    sin = np.tile((np.sin(emb) * sign).T, (HPC, 1)).astype(np.float32)
    at = np.arange(T, dtype=np.float32)
    return {"cos": cos, "sin": sin, "ident": np.eye(P, dtype=np.float32),
            "iota": np.arange(NA, dtype=np.float32).reshape(1, NA),
            "pos_diff": np.clip(at[None, :] - at[:, None], 0, None).astype(np.float32)}


def lay_out(a):
    on_partitions = lambda w: np.ascontiguousarray(w.reshape(C, P, -1).transpose(1, 0, 2))
    column = lambda v: v.reshape(-1, P).T
    f32 = {k: np.asarray(v) for k, v in a.items()}
    at, xa, ff = (lambda n: f32["L0_attn_" + n]), (lambda n: f32["L0_xattn_" + n]), (lambda n: f32["L0_ffn_" + n])
    out = {"x": f32["x"], **shapes_only_constants()}
    out["ctx"] = np.ascontiguousarray(f32["ctx_1024"].transpose(0, 2, 1).reshape(B, C, P, S))
    for w in WEIGHTS_A + ("wo",):
        out["w_" + w] = on_partitions(at(w).T)
    for w in ("Wq", "Wk", "Wv", "Wo"):
        out["w_x" + w] = on_partitions(xa(w).T)
    out["w_base"] = on_partitions(ff("W_base"))
    out["w_enc"] = np.ascontiguousarray(ff("W_enc").reshape(NA, C, P, HID).transpose(2, 0, 1, 3))
    out["w_dec"] = np.ascontiguousarray(ff("W_dec").transpose(1, 0, 2))
    out["w_down"] = np.ascontiguousarray(ff("W_down").reshape(NA, C, P, R).transpose(0, 2, 1, 3))
    out["w_up"] = ff("W_up")
    out["wd"] = on_partitions(at("wd").T)
    out["bd"] = at("bd").reshape(H, 1)
    out["rows"] = np.stack([at("bg"), at("gamma"), at("beta"), at("bo"), at("bv"), xa("bv"), xa("bo"), ff("b_base")])
    out["cols"] = np.ascontiguousarray(np.concatenate(
        [column(at("bq")), column(at("bk")), column(xa("bq")), column(xa("bk")), column(ff("b_enc")),
         column(ff("b_dec"))], axis=1))
    out["b_down"] = ff("b_down").reshape(NA, R, 1)
    out["b_up"] = ff("b_up")
    out["connected"] = ff("connected_idx").reshape(1, NA)
    return out


def scratch(nc, kind="Internal"):
    mk = lambda name, shape, dt: nc.dram_tensor(name, shape, dt, kind=kind).ap()
    return dict(q1=mk("q1", (2, E, TOK), F16), k1=mk("k1", (2, E, TOK), F16), v1=mk("v1", (B, T, H * VW), F16),
                gate=mk("gate", (B, T, E), F32), x2=mk("x2", (B, T, E), F32))


def build(nc, ins, scr, out, phases="abc"):
    d = {**ins, **scr, "out": out}
    d["w"] = {name[2:]: ap for name, ap in ins.items() if name[:2] == "w_"}
    with ExitStack() as ctx:
        sb = lambda name, shape, dt: ctx.enter_context(nc.sbuf_tensor(name, shape, dt))
        keep = Names()
        keep.ident = sb("ident", [P, P], F32)
        keep.pd = sb("pd", [T, T], F32)
        keep.cols = sb("cols", [P, NCOLS], F32)
        keep.ld = sb("ld", [T, B * H], F32)
        with ExitStack() as inner:
            keep.wb = {w: inner.enter_context(nc.sbuf_tensor("k_" + w, [P, 2, C, E], F16)) for w in WEIGHTS_B}
            if "a" in phases:
                phase_a(nc, d, keep)
            if "b" in phases:
                phase_b(nc, d, keep)
        if "c" in phases:
            phase_c(nc, d, keep)


def kernel(**inputs):
    import concourse.bacc as bacc
    from concourse.bass_utils import run_bass_kernel_spmd

    arrays = {"in_" + k: v for k, v in lay_out(inputs).items()}
    nc = bacc.Bacc("TRN2", target_bir_lowering=False, num_devices=1)
    ins = {k[3:]: nc.dram_tensor(k, v.shape, mybir.dt.from_np(v.dtype), kind="ExternalInput").ap()
           for k, v in arrays.items()}
    out = nc.dram_tensor("out", (B, T, E), F32, kind="ExternalOutput").ap()
    build(nc, ins, scratch(nc), out)
    r = run_bass_kernel_spmd(nc, [arrays], core_ids=[0])
    return r.results[0]["out"]
```

```python
from contextlib import ExitStack

import numpy as np

import concourse.bass as bass
from concourse import mybir

F32 = mybir.dt.float32
F16 = mybir.dt.float16
I32 = mybir.dt.int32
ALU = mybir.AluOpType
ACT = mybir.ActivationFunctionType
AX = mybir.AxisListType

B, T, E = 8, 100, 512
H, HD = 16, 32
S = 722
P = 128
C = E // P
HPC = P // HD
NA, HID, R = 8, 128, 64
HALF = B // 2
NT = HALF * T
TOK = B * T
TOKP = TOK + P - T
KT = -(-S // P)
SP_ = KT * P
SH = S // 2
LASTK = S - (KT - 1) * P
VW = 2 * HD + 1
WS = 16.0
SC = 1.0 / (WS * WS * float(np.sqrt(HD)))
MS = 256.0
EPS = 1e-5
MAGIC = 0x5F3759DF
NCOLS = 4 * C + NA + NA * C
QPLANES = (0, 0, 1)
KPLANES = (0, 1, 0)

WEIGHTS_A = ("wq", "wv", "wg", "wk")
WEIGHTS_B = ("wo", "xWq", "xWk", "xWv", "xWo")
ROWS = ("bg", "gamma", "beta", "bo", "bv", "xbv", "xbo", "b_base")
COLS = ("bq", "bk", "xbq", "xbk")


class Chain:

    def __init__(self, eng, sem, per):
        self.eng, self.sem, self.per, self.item, self.n = eng, sem, per, 0, 0

    def start(self, item):
        self.item, self.n = item, 0

    def step(self, ins):
        self.n += 1
        assert self.n <= self.per
        ins.then_inc(self.sem, 1)
        self.eng.wait_ge(self.sem, self.item * self.per + self.n)


NEWTON = 3
RSQRT_STEPS = 2 + 4 * NEWTON


def rsqrt_guess(dve, chain, y, t, v):
    chain.step(dve.tensor_single_scalar(t.bitcast(I32), v.bitcast(I32), 1, ALU.logical_shift_right))
    chain.step(dve.tensor_scalar(y.bitcast(I32), t.bitcast(I32), -1.0, float(MAGIC), ALU.mult, ALU.add))


def newton(dve, chain, y, t, v):
    chain.step(dve.tensor_tensor(t, y, y, ALU.mult))
    chain.step(dve.tensor_tensor(t, t, v, ALU.mult))
    chain.step(dve.tensor_scalar(t, t, -0.5, 1.5, ALU.mult, ALU.add))
    chain.step(dve.tensor_tensor(y, y, t, ALU.mult))


def rsqrt(dve, chain, y, t, v):
    rsqrt_guess(dve, chain, y, t, v)
    for _ in range(NEWTON):
        newton(dve, chain, y, t, v)


def phase_a(nc, d, keep):
    with ExitStack() as ctx:
        sb = lambda name, shape, dt: ctx.enter_context(nc.sbuf_tensor("a_" + name, shape, dt))
        sem = lambda name: ctx.enter_context(nc.semaphore("a_" + name))
        ps = ctx.enter_context(nc.psum_tensor("a_ps", [P, 8, 512], F32))
        NST = 3
        stage = sb("stage", [P, NST, C, E], F32)
        x = sb("x", [T, B, E], F32)
        wa = {w: sb(w, [P, 2, C, E], F16) for w in WEIGHTS_A}
        wsplit = {**wa, **keep.wb}
        nT = sb("nT", [P, 2, C, TOKP], F16)
        ntok = sb("ntok", [T, 2, E], F32)
        bnst = sb("bnst", [T, B, 6], F32)
        mv = sb("mv", [T, B, 2], F32)
        ve = sb("ve", [T, B], F32)
        rstd = sb("rstd", [T, B], F32)
        scr = sb("scr", [T, B], F32)
        cst = sb("cst", [P, 2, S], F32)
        cos = sb("cos", [P, T], F32)
        sin = sb("sin", [P, T], F32)
        bgr = sb("bgr", [P, E], F32)
        qraw = sb("qraw", [P, 2, NT], F32)
        qsw = sb("qsw", [P, 2, NT], F32)
        qcos = sb("qcos", [P, 2, NT], F32)
        qrot = sb("qrot", [P, 2, NT], F32)
        qhl = sb("qhl", [P, 2, 2, NT], F16)
        vbuf = sb("vbuf", [T, 2, H, VW], F16)
        gpre = sb("gpre", [T, 2, E], F32)
        gth = sb("gth", [T, 2, E], F32)
        gout = sb("gout", [T, 2, E], F32)
        nmean = sb("nmean", [P, C, B], F32)
        wdT = sb("wdT", [P, C, H], F32)
        bd = sb("bd", [H, 1], F32)
        dec = sb("dec", [H, 4, B], F32)
        decx = sb("decx", [H, B, H], F32)
        ones = sb("ones", [H, P], F32)

        s_x = [sem(f"x_in{i}") for i in range(B // 2)]
        s_ident = sem("ident_in")
        s_cst = [sem(f"context_in{i}") for i in range(2)]
        s_chi, s_clo = sem("context_hi"), sem("context_lo")
        s_w = [sem(f"stage_in{i}") for i in range(NST)]
        s_const = sem("const_in")
        s_whi = sem("weights_hi")
        s_wlo = sem("weights_lo")
        s_init = sem("init")
        s_bn = sem("bn_stats")
        s_mv = sem("bn_aggr")
        s_rs = sem("rstd_chain")
        s_ntok = sem("normed")
        s_tp = sem("transposed")
        s_nhi = sem("nT_hi")
        s_nlo = sem("nT_lo")
        s_qk = sem("qk_product")
        s_raw = sem("qk_raw")
        s_sw = sem("qk_swapped")
        s_sn = sem("qk_sin")
        s_cs = sem("qk_cos")
        s_rot = sem("qk_rotated")
        s_qhi = sem("qk_hi")
        s_qlo = sem("qk_lo")
        s_qout = [sem(f"qk_stored{i}") for i in range(2)]
        s_v = sem("v_product")
        s_vhi = sem("v_hi")
        s_vlo = sem("v_lo")
        s_vout = [sem(f"v_stored{i}") for i in range(2)]
        s_g = sem("gate_product")
        s_gpre = sem("gate_biased")
        s_gth = sem("gate_tanh")
        s_gout = sem("gate_done")
        s_gst = [sem(f"gate_stored{i}") for i in range(2)]
        s_dp = sem("decay_product")
        s_da = sem("decay_act")
        s_dv = sem("decay_vec")

        NW = len(wsplit)
        ALLW = list(wsplit)
        QK = [(w, oc, hf) for hf in range(2) for w in range(2) for oc in range(C)]
        NQ = len(QK)
        values_of = lambda u: (u - 3) // 2 if u % 2 and u >= 3 else None
        BESIDES = {0: (1, None), 1: (2, 4), 2: (None, 5), 3: (3, 6), 4: (None, 7), 6: (4, None), 8: (5, None),
                   10: (6, None), 11: (7, None), 13: (8, None)}
        later = lambda u: BESIDES.get(u, (None, None))
        later_context = lambda u: (u - 5) // 2 if u % 2 and 5 <= u < 5 + 2 * C else None
        DECAY = 8
        qk_dram = (d["q1"], d["k1"])
        block = ctx.enter_context(nc.Block())

        @block.sync
        def _(sp):
            for i in range(B // 2):
                sp.dma_start(x[:, 2 * i:2 * i + 2], d["x"][2 * i:2 * i + 2].rearrange("b t f -> t b f")).then_inc(s_x[i], 16)
            sp.dma_start(keep.ident[:, :], d["ident"]).then_inc(s_ident, 16)

            def weight(i):
                if i >= NST:
                    sp.wait_ge(s_wlo, i - NST + 1)
                sp.dma_start(stage[:, i % NST], d["w"][ALLW[i]]).then_inc(s_w[i % NST], 16)

            def store(b):
                sp.wait_ge(s_vlo, b + 1)
                sp.dma_start(d["v1"][b], vbuf[:, b % 2].rearrange("t h w -> t (h w)")).then_inc(s_vout[b % 2], 16)
                sp.wait_ge(s_gout, b + 1)
                sp.dma_start(d["gate"][b], gout[:, b % 2]).then_inc(s_gst[b % 2], 16)

            def context(c):
                if c >= 2:
                    sp.wait_ge(s_clo, c - 1)
                sp.dma_start(cst[:, c % 2], d["ctx"][0, c]).then_inc(s_cst[c % 2], 16)

            for i in range(NST):
                weight(i)
            for c in range(2):
                context(c)
            for u, (w, oc, hf) in enumerate(QK):
                if later(u)[0] is not None and later(u)[0] + NST - 1 < NW:
                    weight(later(u)[0] + NST - 1)
                sp.wait_ge(s_qlo, u + 1)
                for pl in range(2):
                    sp.dma_start(qk_dram[w][pl, oc * P:(oc + 1) * P, hf * NT:(hf + 1) * NT],
                                 qhl[:, u % 2, pl, :]).then_inc(s_qout[u % 2], 16)
                if values_of(u - 1) is not None:
                    store(values_of(u - 1))
                if later_context(u) is not None and later_context(u) + 2 < C:
                    context(later_context(u) + 2)
            store(B - 2)
            store(B - 1)
            for i in range(2):
                sp.wait_ge(s_qout[i], 16 * NQ)
                sp.wait_ge(s_vout[i], 8 * B)
                sp.wait_ge(s_gst[i], 8 * B)

        @block.gpsimd
        def _(pool):
            for dst, src in ((cos[:, :], d["cos"]), (sin[:, :], d["sin"]),
                             (keep.pd[:, :], d["pos_diff"]), (keep.cols[:, :], d["cols"]),
                             (wdT[:, :, :], d["wd"]), (bd[:, :], d["bd"]), (bgr[:, :], d["rows"][0:1, :].broadcast_to((P, E)))):
                pool.dma_start(dst, src).then_inc(s_const, 16)
            pool.memset(nT[:, :, :, TOK:TOKP], 0.0).then_inc(s_init, 1)
            pool.memset(vbuf[:, :, :, HD:HD + 1], WS).then_inc(s_init, 1)
            pool.memset(ones[:, :], 1.0).then_inc(s_init, 1)
            pool.wait_ge(s_const, 16 * 7)
            for u in range(NQ):
                pool.wait_ge(s_raw, u + 1)
                if u >= 2:
                    pool.wait_ge(s_rot, u - 1)
                pool.tensor_tensor(qcos[:, u % 2].rearrange("p (b t) -> p b t", t=T),
                                   qraw[:, u % 2].rearrange("p (b t) -> p b t", t=T),
                                   cos[:, None, :].broadcast_to((P, HALF, T)), ALU.mult).then_inc(s_cs, 1)
                if u >= 1:
                    pool.wait_ge(s_qhi, u)
                    pool.tensor_tensor(qhl[:, (u - 1) % 2, 1], qrot[:, (u - 1) % 2], qhl[:, (u - 1) % 2, 0],
                                       ALU.subtract).then_inc(s_qlo, 1)
                if later_context(u) is not None:
                    c = later_context(u)
                    pool.wait_ge(s_chi, c + 1)
                    pool.tensor_tensor(keep.ch[:, 0, 1, c], cst[:, c % 2], keep.ch[:, 0, 0, c], ALU.subtract).then_inc(s_clo, 1)
            pool.wait_ge(s_qhi, NQ)
            pool.tensor_tensor(qhl[:, (NQ - 1) % 2, 1], qrot[:, (NQ - 1) % 2], qhl[:, (NQ - 1) % 2, 0],
                               ALU.subtract).then_inc(s_qlo, 1)

        @block.scalar
        def _(act):
            def weight_hi(i):
                act.wait_ge(s_w[i % NST], 16 * (i // NST + 1))
                act.activation(wsplit[ALLW[i]][:, 0], stage[:, i % NST], ACT.Copy, scale=WS).then_inc(s_whi, 1)

            def turned_hi(b):
                act.wait_ge(s_tp, b + 1)
                act.activation(nT[:, 0, :, b * T:(b + 1) * T],
                               ps[:, b % 2, 0:C * T].rearrange("p (c t) -> p c t", t=T), ACT.Copy).then_inc(s_nhi, 1)

            weight_hi(0)
            for b in range(HALF):
                turned_hi(b)
            act.wait_ge(s_const, 16 * 7)
            act.wait_ge(s_dv, 1)

            def context_hi(c):
                act.wait_ge(s_cst[c % 2], 16 * (c // 2 + 1))
                act.activation(keep.ch[:, 0, 0, c], cst[:, c % 2], ACT.Copy).then_inc(s_chi, 1)

            def raw(u):
                w, oc, hf = QK[u]
                act.wait_ge(s_qk, u + 1)
                if u >= 2:
                    act.wait_ge(s_cs, u - 1)
                    act.wait_ge(s_sw, u - 1)
                act.activation(qraw[:, u % 2], ps[:, 2 + u % 2, 0:NT], ACT.Identity,
                               bias=keep.cols[:, w * C + oc:w * C + oc + 1]).then_inc(s_raw, 1)

            def hi(u):
                act.wait_ge(s_rot, u + 1)
                if u >= 2:
                    act.wait_ge(s_qout[u % 2], 32 * (u // 2))
                act.activation(qhl[:, u % 2, 0], qrot[:, u % 2], ACT.Copy).then_inc(s_qhi, 1)

            def values_hi(b):
                act.wait_ge(s_v, b + 1)
                if b >= 2:
                    act.wait_ge(s_vout[b % 2], 16 * (b // 2))
                act.wait_ge(s_init, 3)
                act.activation(vbuf[:, b % 2, :, 0:HD], ps[0:T, 4 + b % 2, :].rearrange("t (h w) -> t h w", w=HD),
                               ACT.Copy).then_inc(s_vhi, 1)

            def tanh(b):
                act.wait_ge(s_gpre, b + 1)
                if b >= 2:
                    act.wait_ge(s_gout, b - 1)
                act.activation(gth[:, b % 2], gpre[:, b % 2], ACT.Tanh, scale=0.5).then_inc(s_gth, 1)

            def decay(step):
                if step == 2:
                    act.wait_ge(s_dp, 1)
                    act.wait_ge(s_dv, 2)
                    act.activation(dec[:, 1], dec[:, 0], ACT.Exp, scale=-1.0).then_inc(s_da, 1)
                elif step == 3:
                    act.wait_ge(s_dv, 4)
                    act.activation(dec[:, 3], dec[:, 2], ACT.Exp, scale=-8.0 * float(np.log(2.0)),
                                   bias=0.0).then_inc(s_da, 1)
                elif step == 4:
                    act.wait_ge(s_dv, 5)
                    act.activation(dec[:, 1], dec[:, 0], ACT.Ln).then_inc(s_da, 1)

            for u in range(NQ):
                raw(u)
                if values_of(u - 1) is not None:
                    tanh(values_of(u - 1))
                if u >= 1:
                    hi(u - 1)
                if values_of(u) is not None:
                    values_hi(values_of(u))
                if later(u - 2)[1] is not None:
                    turned_hi(later(u - 2)[1])
                if later(u)[0] is not None:
                    weight_hi(later(u)[0])
                if later_context(u) is not None:
                    context_hi(later_context(u))
                decay(u - DECAY)
            hi(NQ - 1)
            values_hi(B - 1)
            tanh(B - 2)
            tanh(B - 1)

        def lo_and_mean(dve, b):
            src = ps[:, b % 2, 0:C * T].rearrange("p (c t) -> p c t", t=T)
            dve.wait_ge(s_nhi, b + 1)
            dve.tensor_reduce(nmean[:, :, b], src, AX.X, ALU.add)
            dve.tensor_tensor(nT[:, 1, :, b * T:(b + 1) * T], src, nT[:, 0, :, b * T:(b + 1) * T],
                              ALU.subtract).then_inc(s_nlo, 1)

        @block.vector
        def _(dve):
            chain = Chain(dve, s_rs, 1 + RSQRT_STEPS)

            def weight_lo(i):
                dve.wait_ge(s_whi, i + 1)
                w = wsplit[ALLW[i]]
                dve.scalar_tensor_tensor(out=w[:, 1], in0=stage[:, i % NST], scalar=WS, in1=w[:, 0],
                                         op0=ALU.mult, op1=ALU.subtract).then_inc(s_wlo, 1)

            def normed(b):
                if b >= 2:
                    dve.wait_ge(s_tp, b - 1)
                dve.tensor_scalar(ntok[:, b % 2], x[:, b], mv[:, b, 0:1], rstd[:, b:b + 1],
                                  ALU.subtract, ALU.mult).then_inc(s_ntok, 1)

            for b in range(B):
                dve.wait_ge(s_x[b // 2], 16)
                dve.bn_stats(bnst[:, b], x[:, b]).then_inc(s_bn, 1)
            for b in range(B):
                dve.wait_ge(s_bn, b + 1)
                dve.bn_aggr(mv[:, b], bnst[:, b]).then_inc(s_mv, 1)
            dve.wait_ge(s_mv, B)
            chain.start(0)
            chain.step(dve.tensor_scalar(ve[:, :], mv[:, :, 1], EPS, None, ALU.add))
            rsqrt(dve, chain, rstd[:, :], scr[:, :], ve[:, :])
            for b in range(HALF):
                normed(b)
                if b == 0:
                    weight_lo(0)
                else:
                    lo_and_mean(dve, b - 1)
            lo_and_mean(dve, HALF - 1)
            dve.wait_ge(s_const, 16 * 7)
            dve.tensor_scalar(keep.cols[:, :], keep.cols[:, :], WS, None, ALU.mult).then_inc(s_dv, 1)

            def rotate(u):
                dve.wait_ge(s_raw, u + 1)
                dve.stream_shuffle(qsw[:, u % 2], qraw[:, u % 2], [i ^ 1 for i in range(32)]).then_inc(s_sw, 1)
                dve.wait_ge(s_sw, u + 1)
                v = qsw[:, u % 2].rearrange("p (b t) -> p b t", t=T)
                dve.tensor_tensor(v, v, sin[:, None, :].broadcast_to((P, HALF, T)), ALU.mult).then_inc(s_sn, 1)
                dve.wait_ge(s_sn, u + 1)
                dve.wait_ge(s_cs, u + 1)
                if u >= 2:
                    dve.wait_ge(s_qlo, u - 1)
                dve.tensor_tensor(qrot[:, u % 2], qsw[:, u % 2], qcos[:, u % 2], ALU.add).then_inc(s_rot, 1)

            def values_lo(b):
                dve.wait_ge(s_vhi, b + 1)
                dve.tensor_tensor(vbuf[:, b % 2, :, HD + 1:VW], ps[0:T, 4 + b % 2, :].rearrange("t (h w) -> t h w", w=HD),
                                  vbuf[:, b % 2, :, 0:HD], ALU.subtract).then_inc(s_vlo, 1)

            def gate_biased(b):
                dve.wait_ge(s_g, b + 1)
                if b >= 2:
                    dve.wait_ge(s_gout, b - 1)
                dve.scalar_tensor_tensor(out=gpre[:, b % 2], in0=ps[0:T, 6 + b % 2, :], scalar=1.0 / WS,
                                         in1=bgr[0:T], op0=ALU.mult, op1=ALU.add).then_inc(s_gpre, 1)

            def gate(b):
                dve.wait_ge(s_gth, b + 1)
                if b >= 2:
                    dve.wait_ge(s_gst[b % 2], 16 * (b // 2))
                dve.scalar_tensor_tensor(out=gout[:, b % 2], in0=gth[:, b % 2], scalar=1.0, in1=gpre[:, b % 2],
                                         op0=ALU.add, op1=ALU.mult).then_inc(s_gout, 1)

            def decay(step):
                if step == 1:
                    dve.wait_ge(s_dp, 1)
                    dve.tensor_scalar(dec[:, 0], ps[0:H, 0, 0:B], 1.0 / T, bd[:, 0:1], ALU.mult, ALU.add).then_inc(s_dv, 1)
                elif step == 2:
                    dve.wait_ge(s_da, 1)
                    dve.tensor_scalar(dec[:, 1], dec[:, 1], 1.0, None, ALU.add).then_inc(s_dv, 1)
                    dve.wait_ge(s_dv, 3)
                    dve.reciprocal(dec[:, 2], dec[:, 1]).then_inc(s_dv, 1)
                elif step == 3:
                    dve.wait_ge(s_da, 2)
                    dve.tensor_scalar(dec[:, 0], dec[:, 3], -1.0 / 32.0, 1.0, ALU.mult, ALU.add).then_inc(s_dv, 1)
                elif step == 4:
                    dve.wait_ge(s_da, 3)
                    dve.tensor_scalar(dec[:, 2], dec[:, 1], 1.0 / SC, None, ALU.mult).then_inc(s_dv, 1)
                    dve.wait_ge(s_dv, 6)
                    dve.tensor_tensor(decx[:, :, :], keep.ident[0:H, None, 0:H].broadcast_to((H, B, H)),
                                      dec[:, 2, :, None].broadcast_to((H, B, H)), ALU.mult).then_inc(s_dv, 1)
                elif step == 6:
                    dve.wait_ge(s_dp, 2)
                    dve.tensor_copy(keep.ld[:, :], ps[0:T, 1, 0:B * H]).then_inc(s_dv, 1)

            for u in range(NQ):
                if values_of(u - 1) is not None:
                    gate_biased(values_of(u - 1))
                rotate(u)
                if values_of(u) is not None:
                    values_lo(values_of(u))
                if values_of(u - 1) is not None:
                    gate(values_of(u - 1))
                if later(u - 2)[1] is not None:
                    lo_and_mean(dve, later(u - 2)[1])
                load, b = later(u)
                if b is not None:
                    normed(b)
                if load is not None:
                    weight_lo(load)
                decay(u - DECAY)
            gate_biased(B - 2)
            values_lo(B - 1)
            gate(B - 2)
            gate_biased(B - 1)
            gate(B - 1)

        @block.tensor
        def _(pe):
            def turn(b):
                pe.wait_ge(s_ntok, b + 1)
                if b >= 2:
                    pe.wait_ge(s_nlo, b - 1)
                for c in range(C):
                    mm = pe.transpose(ps[:, b % 2, c * T:(c + 1) * T], ntok[:, b % 2, c * P:(c + 1) * P],
                                      keep.ident[0:T, 0:T])
                mm.then_inc(s_tp, 1)

            pe.wait_ge(s_ident, 16)
            for b in range(HALF):
                turn(b)

            def qk(u):
                w, oc, hf = QK[u]
                if u >= 2:
                    pe.wait_ge(s_raw, u - 1)
                wt = wa[("wq", "wk")[w]]
                pe.wait_ge(s_wlo, ALLW.index(("wq", "wk")[w]) + 1)
                pe.wait_ge(s_nlo, HALF * (hf + 1))
                passes(pe, ps[:, 2 + u % 2, 0:NT], lambda pl, c: wt[:, pl, c, oc * P:(oc + 1) * P],
                       lambda pl, c: nT[:, pl, c, hf * NT:(hf + 1) * NT]).then_inc(s_qk, 1)

            def vg(b):
                pe.wait_ge(s_wlo, ALLW.index("wg") + 1)
                pe.wait_ge(s_nlo, min(b + 2, B))
                pe.wait_ge(s_init, 3)
                window = lambda pl, c: nT[:, pl, c, b * T:b * T + P]
                if b >= 2:
                    pe.wait_ge(s_vlo, b - 1)
                passes(pe, ps[:, 4 + b % 2, :], window, lambda pl, c: wa["wv"][:, pl, c, :]).then_inc(s_v, 1)
                if b >= 2:
                    pe.wait_ge(s_gpre, b - 1)
                passes(pe, ps[:, 6 + b % 2, :], window, lambda pl, c: wa["wg"][:, pl, c, :]).then_inc(s_g, 1)

            def decay(step):
                if step == 0:
                    pe.wait_ge(s_nlo, B)
                    pe.wait_ge(s_const, 16 * 7)
                    for c in range(C):
                        mm = pe.matmul(ps[0:H, 0, 0:B], wdT[:, c, :], nmean[:, c, :], start=(c == 0), stop=(c == C - 1))
                    mm.then_inc(s_dp, 1)
                elif step == 5:
                    pe.wait_ge(s_dv, 7)
                    pe.matmul(ps[:, 1, 0:B * H], ones[:, :], decx[:, :, :].rearrange("g b h -> g (b h)"),
                              start=True, stop=True).then_inc(s_dp, 1)

            for u in range(NQ):
                qk(u)
                if values_of(u) is not None:
                    vg(values_of(u))
                if later(u - 1)[1] is not None:
                    turn(later(u - 1)[1])
                decay(u - DECAY)
            vg(B - 1)


PASSES = ((0, 0), (0, 1), (1, 0))


def passes(pe, out, stationary, moving, chunks=C, start=True, stop=True):
    steps = [(c, a, b) for c in range(chunks) for a, b in PASSES]
    for i, (c, a, b) in enumerate(steps):
        mm = pe.matmul(out, stationary(a, c), moving(b, c), start=(start and i == 0),
                       stop=(stop and i == len(steps) - 1))
    return mm


class Names:
    pass


ORDER = """
    v0 tnorm0 tnorm1 sscore0 v1 M0 sscore1 sscore2 M1 sscore3
    k0 ssoft0 M2 k1 ttrans0 ssoft1 M3 k2 ssoft2 X0
    M4 tproj0 c0 ssoft3 W0 M5 strans0 k3 S0
    M6 c1 strans1 v2 S1
    sout0 M7 O0 strans2 sout1 c2 M8 X1 strans3 S2
    k4 W1 S3
    O1 c3 M9 O2 sout2 sout3 snorm0 M10 S4
    v3 O3 snorm1 M11 S5
    O4 k5 smean0 c4 sdev0 O5 S6
    X2 c5 svar0 S7
    M12 W2 snewton0 k6 M13 snewton1 O6 S8
    M14 S9
    c6 O7 snewton2 O8 S10
    M15 X3 v4 sgate0 sturn0 O9 O10 W3 S11
    sproj0 O11 S12
    S13
    nnewton0 nnewton1 k7 nnewton2 O12 c7 O13 S14
    nturn0 v5 S15
    nproj0 O14 O15
""".split()
FIRST_ORDER = """
    v0 v1 sscore0 sscore1 sscore2 sscore3 c0 ssoft0 k0 k1
    ssoft1 c1 k2 k3 strans0 c2 sout0 ssoft2 ssoft3 v2
    strans1 strans2 c3 sout1 strans3 v3 sout2 sout3 snorm0 snorm1
    c4 v4 smean0 sdev0 c5 svar0 snewton0 snewton1 c6 snewton2
    sgate0 k4 c7 sturn0 k5 sproj0 nnewton0 k6 k7 nnewton1
    nnewton2 v5 nturn0 nproj0
""".split()
LAST_ORDER = """
    M0 M1 tnorm0 M2 tnorm1 M3 X0 M4 ttrans0 W0
    M5 S0 M6 tproj0 S1 M7 X1 O0 S2 M8 W1 O1 S3
    M9 O2 S4 M10 O3 S5 M11 X2 O4 S6 M12 W2 O5 S7
    M13 O6 S8 M14 O7 S9 M15 X3 O8 S10 W3 O9 S11
    O10 S12 O11 S13 O12 S14 O13 S15 O14 O15
""".split()
GROUP = HPC
NG = H // GROUP
PJ_TASKS = ("k", "v", "sscore", "strans", "sout", "smean", "svar", "sturn", "sproj", "nturn", "nproj",
            "ttrans", "tproj")
NKU, NVU, NCX = 2 * C, KT, 2 * C
KST_DMAS, QST_DMAS, QK1_DMAS = 3 * HPC, 3, 3


def schedule(order, cross, nxt, nxt2, tail):
    has = {"M": cross, "X": cross, "W": cross, "O": cross, "S": cross, "t": tail, "c": nxt2, "k": nxt, "v": nxt, "s": nxt, "n": nxt}
    split = [(word.rstrip("0123456789"), word) for word in order]
    return [(name, int(word[len(name):])) for name, word in split if has[name[0]]]


def places(tasks, kinds, each):
    at, n = {}, 0
    for task in tasks:
        if task[0] in kinds:
            at[task] = n
            n += each.get(task[0], 1)
    return at, n


class Iteration:

    def __init__(self, b, par, cross=True, nxt=True, nxt2=True, tail=True, order=ORDER):
        self.b, self.par = b, par
        self.tasks = schedule(order, cross, nxt, nxt2, tail)
        self.n, self.npar = b + 1, (par + 1) % 2
        self.pj, self.pj_n = places(self.tasks, PJ_TASKS, {})
        self.st, self.st_n = places(self.tasks, ("W", "S"), {"S": 2})


    def reused(self, task, by):
        again = [t for t, use in self.pj.items() if use == self.pj[task] + 2]
        return bool(again) and self.tasks.index(again[0]) < self.tasks.index(by)


FULL = Iteration(1, 1)
FIRST = [Iteration(-1, 1, cross=False, tail=False, order=FIRST_ORDER), Iteration(0, 0, tail=False), Iteration(1, 1)]
LOOP_FROM, LOOP_TO = 2, 6
LAST = [Iteration(6, 0, nxt2=False), Iteration(7, 1, nxt=False, nxt2=False, order=LAST_ORDER),
        Iteration(8, 0, cross=False, nxt=False, nxt2=False)]


def before(it):
    last = [i for i in FIRST + LAST if isinstance(it.b, int) and i.b == it.b - 1]
    return list((last[0] if last else FULL).pj)


def pj_base(it):
    if isinstance(it.b, int):
        return sum(i.pj_n for i in FIRST if i.b < it.b) + FULL.pj_n * max(0, min(it.b - LOOP_FROM, LOOP_TO - LOOP_FROM)) \
            + sum(i.pj_n for i in LAST if i.b < it.b)
    return it.b * FULL.pj_n + (sum(i.pj_n for i in FIRST) - LOOP_FROM * FULL.pj_n)


def run(eng, body):
    for it in FIRST:
        body(it)
    with eng.Fori(LOOP_FROM, LOOP_TO - 1, 2) as b:
        body(Iteration(b, LOOP_FROM % 2))
        body(Iteration(b + 1, (LOOP_FROM + 1) % 2))
    for it in LAST:
        body(it)


def phase_b(nc, d, keep):
    assert FULL.pj_n % 2 == 0 and FULL.st_n % 3 == 0 and all(i.pj_n % 2 == 0 for i in FIRST + LAST)
    with ExitStack() as ctx:
        sb = lambda name, shape, dt: ctx.enter_context(nc.sbuf_tensor("b_" + name, shape, dt))
        sem = lambda name: ctx.enter_context(nc.semaphore("b_" + name))
        ps = ctx.enter_context(nc.psum_tensor("b_ps", [P, 8, 512], F32))
        PJ, ST, MX, PV = 0, 2, 5, 7
        wb = keep.wb
        ident, cols = keep.ident, keep.cols
        ident16 = sb("ident16", [T, T], F16)
        rows = {r: sb(r, [T, E], F32) for r in ("gamma", "beta", "bo", "bv", "xbv", "xbo")}
        mean_w = sb("mean_w", [T, P], F32)
        cst = sb("cst", [P, 2, SH], F32)
        ch = keep.ch
        keys = sb("keys", [P, C, 2, S], F16)
        kst = sb("kst", [P, H, SP_], F16)
        v2 = sb("v2", [P, 2, KT, H, VW], F16)
        qst = sb("qst", [P, 2, H, P], F16)
        mx = sb("mx", [T, H], F32)
        wrow = sb("wrow", [T, GROUP, P], F16)
        p32 = sb("p32", [P, 3, KT // 2, T], F32)
        ph = sb("ph", [P, 2, KT, P], F16)
        pl = sb("pl", [P, 2, KT, P], F16)
        osb = sb("osb", [T, H, VW], F32)
        x1 = sb("x1", [T, 2, E], F32)
        q1 = sb("q1", [P, H, P], F16)
        k1 = sb("k1", [P, H, P], F16)
        v1 = sb("v1", [T, H, VW], F16)
        gate = sb("gate", [T, E], F32)
        xr = sb("xr", [T, E], F32)
        sc = sb("sc", [T, H, T], F32)
        mx1 = sb("mx1", [T, H], F32)
        sph = sb("sph", [T, 2, GROUP, P], F16)
        spl = sb("spl", [T, 2, GROUP, P], F16)
        sraw = sb("sraw", [T, H, VW], F32)
        og = sb("og", [T, H, HD], F32)
        tmp = sc[:, :, :].rearrange("t h k -> t (h k)")[:, 0:E].rearrange("t (h w) -> t h w", w=HD)
        small = sb("small", [T, 6, H], F32)
        bn = sb("bn", [T, 6], F32)
        mv = sb("mv", [T, 2], F32)
        ln = sb("ln", [T, 3], F32)
        turned = sb("turned", [P, 2, C, P], F16)
        q2 = sb("q2", [P, 2, C, T], F16)
        o2 = sb("o2", [T, H, HD], F32)
        rec2 = sb("rec2", [T, H], F32)
        oturned = sb("oturned", [P, 2, C, P], F16)
        x2 = sb("x2", [T, E], F32)

        s_const, s_init, s_initd = sem("rows_in"), sem("init"), sem("init_dve")
        s_cst = [sem(f"context_in{i}") for i in range(2)]
        s_chi, s_clo = sem("context_hi"), sem("context_lo")
        pj_ready = sem("projection_ready")
        s_khi, s_klo = sem("keys_hi"), sem("keys_lo")
        s_kst = [sem(f"key_stack_in{pair}") for pair in range(2)]
        s_vhi, s_vlo = sem("values_hi"), sem("values_lo")
        s_qst = [sem(f"query_stack_in{r}") for r in range(HPC)]
        mx_ready, mx_done, w_ready = sem("max_scores"), sem("maxima"), sem("maxima_spread")
        st_ready, st_free = sem("scores_ready"), sem("scores_used")
        s_p32, s_pl = sem("probs"), sem("probs_lo")
        pv_done, pv_free = sem("output_done"), sem("output_bank_free")
        s_tch, s_thi, s_tlo = sem("tail_chain"), sem("tail_hi"), sem("tail_lo")
        s_x1b = sem("x1_with_bias")
        s_x2, s_x2out = sem("x2"), sem("x2_stored")
        s_self = [sem(n) for n in ("self_q_in", "self_k_in", "self_v_in", "self_gate_in", "self_x_in")]
        s_bias, s_smax, s_ssub, s_sexp = sem("self_biased"), sem("self_max"), sem("self_shifted"), sem("self_probs")
        s_shi, s_slo, s_sout = sem("self_probs_hi"), sem("self_probs_lo"), sem("self_output")
        s_nch, s_mch = sem("self_norm_chain"), sem("self_group_norm_chain")
        s_scaled, s_affine, s_gated = sem("self_scaled"), sem("self_affine"), sem("self_gated")
        s_gam = sem("self_times_gamma")
        s_xb = sem("x_with_bias")
        s_ghi, s_glo = sem("self_turned_hi"), sem("self_turned_lo")
        s_x1, s_lch, s_n2 = sem("x1"), sem("ln2_chain"), sem("ln2")
        s_nhi, s_nlo, s_q2hi, s_q2lo = sem("ln2_turned_hi"), sem("ln2_turned_lo"), sem("query_hi"), sem("query_lo")
        NORM_STEPS, GROUP_STEPS, LN_STEPS, TAIL_STEPS = 5, 5 + RSQRT_STEPS, 3 + RSQRT_STEPS, 4
        block = ctx.enter_context(nc.Block())

        is_first = lambda b: isinstance(b, int) and b == 0

        def after(eng, s, value, least=1):
            if not isinstance(value, int) or value >= least:
                eng.wait_ge(s, value)

        @block.sync
        def _(sp):

            def context(m, piece):
                c, hf = piece // 2, piece % 2
                after(sp, s_clo, NCX * (m - 1) + piece - 1)
                sp.dma_start(cst[:, hf], d["ctx"][m, c, :, hf * SH:(hf + 1) * SH]).then_inc(s_cst[hf], 16)

            def key_stack(pair):
                for g in range(3):
                    for r in range(HPC):
                        sp.dma_start(kst[HD * g:HD * (g + 1), 2 * HPC * pair + r:2 * HPC * (pair + 1):HPC, 0:S],
                                     keys[HD * r:HD * (r + 1), 2 * pair:2 * pair + 2, KPLANES[g], :]).then_inc(s_kst[pair], 16)

            def self_stacks(n):
                for g in range(3):
                    for stack, src, planes, s in ((q1, d["q1"], QPLANES, s_self[0]), (k1, d["k1"], KPLANES, s_self[1])):
                        sp.dma_start(stack[HD * g:HD * (g + 1), :, 0:T],
                                     src[planes[g], :, bass.ds(n * T, T)].rearrange("(h w) t -> w h t", w=HD)).then_inc(s, 16)

            def self_values(n):
                sp.dma_start(v1[:, :, :], d["v1"][n].rearrange("t (h w) -> t h w", w=VW)).then_inc(s_self[2], 16)

            def self_gate(n):
                sp.dma_start(gate[:, :], d["gate"][n]).then_inc(s_self[3], 16)

            def self_x(n):
                sp.dma_start(xr[:, :], d["x"][n]).then_inc(s_self[4], 16)

            self_stacks(0)
            self_values(0)
            self_gate(0)
            self_x(0)
            for name, r in (("gamma", 1), ("beta", 2), ("bo", 3), ("bv", 4), ("xbv", 5), ("xbo", 6)):
                sp.dma_start(rows[name][:, :], d["rows"][r:r + 1, :].broadcast_to((T, E))).then_inc(s_const, 16)
            def body(it):
                if ("c", 0) in it.tasks:
                    context(it.b + 2, 0)
                if is_first(it.b):
                    sp.wait_ge(s_klo, NKU)
                    key_stack(1)
                elif ("M", 0) in it.tasks:
                    assert FULL.reused(("k", NKU - 1), ("O", H - 1))
                    sp.wait_ge(pv_done, H * it.b)
                    key_stack(1)
                for task, arg in it.tasks:
                    if task == "c":
                        if arg + 1 < NCX:
                            context(it.b + 2, arg + 1)
                    elif (task, arg) == ("k", NKU // 2 - 1) and ("O", 0) not in it.tasks:
                        sp.wait_ge(s_klo, NKU * it.n + arg + 1)
                        key_stack(0)
                    elif (task, arg) == ("O", H // 2 - 1) and ("k", 0) in it.pj:
                        assert it.reused(("k", NKU // 2 - 1), (task, arg))
                        sp.wait_ge(pv_done, H * it.b + arg + 1)
                        key_stack(0)
                    elif ("tproj", 0) in it.pj and (task, arg) == (("S", 0) if ("S", 0) in it.st else ("tproj", 0)):
                        sp.wait_ge(s_x2, it.b)
                        sp.dma_start(d["x2"][it.b - 1], x2[:, :]).then_inc(s_x2out, 16)
                    elif task == "nproj":
                        if is_first(it.b + 1):
                            sp.wait_ge(s_init, 1)
                        sp.wait_ge(s_q2lo, C * it.n + C)
                        for r in range(HPC):
                            for g in range(3):
                                sp.dma_start(qst[HD * g:HD * (g + 1), it.npar, r:H:HPC, 0:T],
                                             q2[HD * r:HD * (r + 1), QPLANES[g], :, :]).then_inc(s_qst[r], 16)
                    elif ("c", 0) not in it.tasks:
                        continue
                    elif (task, arg) == ("snorm", 0):
                        sp.wait_ge(pj_ready, pj_base(it) + it.pj[("sscore", NG - 1)] + 1)
                        self_stacks(it.n + 1)
                    elif task == "svar":
                        sp.wait_ge(s_sout, NG * (it.n + 1))
                        self_values(it.n + 1)
                    elif task == "sturn":
                        sp.wait_ge(s_gated, it.n + 1)
                        self_gate(it.n + 1)
                    elif task == "nturn":
                        sp.wait_ge(s_x1, it.n + 1)
                        self_x(it.n + 1)

            run(sp, body)
            sp.wait_ge(s_x2out, 16 * B)

        @block.gpsimd
        def _(pool):
            pool.memset(qst[:, :, :, :].bitcast(F32), 0.0).then_inc(s_init, 1)
            pool.memset(kst[0:96, :, S:SP_], 0.0).then_inc(s_init, 1)
            pool.wait_ge(s_init, 2)
            two_ms = np.array([MS, MS], np.float16).view(np.float32)[0]
            pool.memset(kst[96:P, :, :].bitcast(F32), float(two_ms)).then_inc(s_init, 1)
            pool.wait_ge(s_init, 3)
            pool.memset(v2[:, :, :, :, HD:HD + 1], WS).then_inc(s_init, 1)

            def split(m, piece, par):
                c, hf = piece // 2, piece % 2
                dst = ch[:, par, :, c, hf * SH:(hf + 1) * SH]
                pool.wait_ge(s_chi, NCX * (m - 1) + piece + 1)
                pool.tensor_tensor(dst[:, 1], cst[:, hf], dst[:, 0], ALU.subtract).then_inc(s_clo, 1)

            def body(it):
                st_base, n = FULL.st_n * it.b, it.n
                for task, arg in it.tasks:
                    if task == "c":
                        split(it.b + 2, arg, it.par)
                    elif task == "S":
                        for t in range(2):
                            pool.wait_ge(st_free, st_base + it.st[("S", arg)] + t + 1)
                            half = slice(t * KT // 2, (t + 1) * KT // 2)
                            pool.tensor_tensor(pl[:, arg % 2, half, 0:T], p32[:, (2 * arg + t) % 3],
                                               ph[:, arg % 2, half, 0:T], ALU.subtract).then_inc(s_pl, 1)
                    elif task == "ssoft" and arg == 0:
                        if is_first(n):
                            pool.wait_ge(s_const, 16 * 6)
                        pool.wait_ge(s_self[4], 16 * (n + 1))
                        pool.tensor_tensor(xr[:, :], xr[:, :], rows["bo"][:, :], ALU.add).then_inc(s_xb, 1)
                    elif (task, arg) == ("snewton", NEWTON - 1):
                        pool.wait_ge(s_scaled, n + 1)
                        flat = og[:, :, :].rearrange("t h w -> t (h w)")
                        pool.tensor_tensor(flat, flat, rows["gamma"][:, :], ALU.mult).then_inc(s_gam, 1)
                        pool.wait_ge(s_gam, n + 1)
                        pool.tensor_tensor(flat, flat, rows["beta"][:, :], ALU.add).then_inc(s_affine, 1)
                    elif task == "nturn":
                        pool.wait_ge(s_n2, n + 1)
                        pool.tensor_tensor(x1[:, it.npar], x1[:, it.npar], rows["xbo"][:, :], ALU.add).then_inc(s_x1b, 1)

            run(pool, body)

        @block.scalar
        def _(act):
            act.wait_ge(s_initd, 5)

            def context_hi(m, piece, par):
                c, hf = piece // 2, piece % 2
                act.wait_ge(s_cst[hf], 16 * (C * (m - 1) + c + 1))
                act.activation(ch[:, par, 0, c, hf * SH:(hf + 1) * SH], cst[:, hf], ACT.Copy).then_inc(s_chi, 1)

            def body(it):
                base, st_base, b, n = pj_base(it), FULL.st_n * it.b, it.b, it.n
                for task, arg in it.tasks:
                    if task == "c":
                        if arg == 0:
                            after(act, s_vlo, NVU * n)
                            after(act, s_klo, NKU * n)
                        context_hi(b + 2, arg, it.par)
                        continue
                    bank = PJ + it.pj.get((task, arg), 0) % 2
                    ready = base + it.pj.get((task, arg), 0) + 1
                    if task == "k":
                        oc, hf = arg // 2, arg % 2
                        act.wait_ge(pj_ready, ready)
                        if hf == 0 and oc % 2 == 0:
                            after(act, s_kst[oc // 2], 16 * KST_DMAS * n)
                        act.activation(keys[:, oc, 0, hf * SH:(hf + 1) * SH], ps[:, bank, 0:SH], ACT.Identity,
                                       bias=cols[:, 3 * C + oc:3 * C + oc + 1]).then_inc(s_khi, 1)
                    elif task == "v":
                        act.wait_ge(pj_ready, ready)
                        if arg == 0:
                            after(act, pv_done, H * b)
                        m = P if arg < KT - 1 else LASTK
                        act.activation(v2[0:m, it.npar, arg, :, 0:HD], ps[0:m, bank, :].rearrange("p (h w) -> p h w", w=HD),
                                       ACT.Copy).then_inc(s_vhi, 1)
                    elif task == "W":
                        act.wait_ge(st_ready, st_base + it.st[(task, arg)] + 1)
                        act.activation(qst[96:97, it.par, GROUP * arg:GROUP * (arg + 1), 0:T],
                                       ps[96:97, ST + it.st[(task, arg)] % 3, 0:GROUP * T].rearrange("p (h t) -> p h t", t=T),
                                       ACT.Copy).then_inc(st_free, 1)
                    elif task == "S":
                        for t in range(2):
                            use = it.st[(task, arg)] + t
                            src = ps[:, ST + use % 3, 0:KT // 2 * T].rearrange("p (k t) -> p k t", t=T)
                            act.wait_ge(st_ready, st_base + use + 1)
                            after(act, s_pl, 2 * H * b + 2 * arg + t - 2)
                            act.activation(p32[:, (2 * arg + t) % 3], src, ACT.Exp, scale=SC).then_inc(s_p32, 1)
                            if t == 0:
                                after(act, pv_done, H * b + arg - 1)
                            act.activation(ph[:, arg % 2, t * KT // 2:(t + 1) * KT // 2, 0:T], src, ACT.Exp,
                                           scale=SC).then_inc(st_free, 1)
                    elif task == "ssoft":
                        act.wait_ge(s_ssub, NG * n + arg + 1)
                        group = sc[:, GROUP * arg:GROUP * (arg + 1)]
                        act.activation(group, group, ACT.Exp, scale=SC).then_inc(s_sexp, 1)
                    elif task == "strans":
                        act.wait_ge(pj_ready, ready)
                        if arg >= 2 or not isinstance(n, int) or n > 0:
                            act.wait_ge(s_sout, NG * n + arg - 1)
                        act.activation(sph[:, arg % 2, :, 0:T], ps[0:T, bank, 0:GROUP * T].rearrange("p (h t) -> p h t", t=T),
                                       ACT.Copy).then_inc(s_shi, 1)
                    elif task in ("sturn", "nturn", "ttrans"):
                        dst, s = {"sturn": (turned, s_ghi), "nturn": (turned, s_nhi), "ttrans": (oturned, s_thi)}[task]
                        act.wait_ge(pj_ready, ready)
                        act.activation(dst[:, 0, :, 0:T], ps[:, bank, 0:C * T].rearrange("p (c t) -> p c t", t=T),
                                       ACT.Copy).then_inc(s, 1)
                    elif task == "nproj":
                        act.wait_ge(pj_ready, ready)
                        for s in s_qst:
                            after(act, s, 16 * QST_DMAS * n)
                        for oc in range(C):
                            act.activation(q2[:, 0, oc], ps[:, bank, oc * T:(oc + 1) * T], ACT.Identity,
                                           bias=cols[:, 2 * C + oc:2 * C + oc + 1]).then_inc(s_q2hi, 1)

            run(act, body)

        @block.vector
        def _(dve):
            dve.memset(wrow[:, :, :].bitcast(F32), 0.0).then_inc(s_initd, 1)
            dve.memset(mean_w[:, :], 1.0 / (T * HD)).then_inc(s_initd, 1)
            dve.tensor_copy(ident16[:, :], ident[0:T, 0:T]).then_inc(s_initd, 1)
            dve.memset(ph[:, :, :, T:P], 0.0).then_inc(s_initd, 1)
            dve.memset(pl[:, :, :, T:P], 0.0)
            dve.memset(sph[:, :, :, T:P], 0.0)
            dve.memset(spl[:, :, :, T:P], 0.0)
            dve.memset(turned[:, :, :, T:P], 0.0)
            dve.memset(oturned[:, :, :, T:P], 0.0)
            dve.memset(q1[:, :, T:P], 0.0)
            dve.memset(k1[:, :, T:P], 0.0).then_inc(s_initd, 1)
            dve.wait_ge(s_initd, 5)
            norm, group = Chain(dve, s_nch, NORM_STEPS), Chain(dve, s_mch, GROUP_STEPS)
            lnorm, tail = Chain(dve, s_lch, LN_STEPS), Chain(dve, s_tch, TAIL_STEPS)
            ogf = og[:, :, :].rearrange("t h w -> t (h w)")
            spread = lambda v: v[:, :, None].broadcast_to((T, H, HD))

            def softmax_out(part, chain, raw, rec, out, bias):
                if part == 0:
                    chain.step(dve.reciprocal(rec, raw[:, :, HD]))
                    chain.step(dve.tensor_tensor(out, raw[:, :, 0:HD], raw[:, :, HD + 1:VW], ALU.add))
                else:
                    chain.step(dve.tensor_tensor(out, out, spread(rec), ALU.mult))
                    chain.step(dve.tensor_tensor(out, out, bias.rearrange("t (h w) -> t h w", w=HD), ALU.add))

            def body(it):
                base, st_base, b, n = pj_base(it), FULL.st_n * it.b, it.b, it.n
                for task, arg in it.tasks:
                    bank = PJ + it.pj.get((task, arg), 0) % 2
                    ready = base + it.pj.get((task, arg), 0) + 1
                    if task == "k":
                        oc, hf = arg // 2, arg % 2
                        cut = slice(hf * SH, (hf + 1) * SH)
                        dve.wait_ge(s_khi, NKU * n + arg + 1)
                        dve.scalar_tensor_tensor(out=keys[:, oc, 1, cut], in0=ps[:, bank, 0:SH],
                                                 scalar=cols[:, 3 * C + oc:3 * C + oc + 1], in1=keys[:, oc, 0, cut],
                                                 op0=ALU.add, op1=ALU.subtract).then_inc(s_klo, 1)
                    elif task == "v":
                        m = P if arg < KT - 1 else LASTK
                        dve.wait_ge(s_vhi, NVU * n + arg + 1)
                        dve.tensor_tensor(v2[0:m, it.npar, arg, :, HD + 1:VW], ps[0:m, bank, :].rearrange("p (h w) -> p h w", w=HD),
                                          v2[0:m, it.npar, arg, :, 0:HD], ALU.subtract).then_inc(s_vlo, 1)
                    elif task == "M":
                        dve.wait_ge(mx_ready, H * b + arg + 1)
                        if arg % GROUP == 0:
                            after(dve, w_ready, NG * (b - 1) + arg // GROUP + 1)
                        dve.tensor_reduce(mx[:, arg:arg + 1], ps[0:T, MX:MX + 2, 0:SH], AX.XY, ALU.max).then_inc(mx_done, 1)
                    elif task == "X":
                        dve.wait_ge(mx_done, H * b + GROUP * (arg + 1))
                        if arg >= 1:
                            dve.wait_ge(st_ready, st_base + it.st[("W", arg - 1)] + 1)
                        else:
                            after(dve, st_ready, st_base)
                        dve.tensor_scalar(wrow[:, :, 96], mx[:, GROUP * arg:GROUP * (arg + 1)], -1.0 / MS, None,
                                          ALU.mult).then_inc(w_ready, 1)
                    elif task == "O":
                        if arg % GROUP == GROUP - 1:
                            g = arg // GROUP
                            dve.wait_ge(pv_done, H * b + arg + 1)
                            if g == 0:
                                after(dve, s_tch, TAIL_STEPS * b)
                            dve.tensor_copy(osb[:, GROUP * g:GROUP * (g + 1)],
                                            ps[0:T, PV, 0:GROUP * VW].rearrange("p (h w) -> p h w", w=VW)).then_inc(pv_free, 1)
                    elif task == "tnorm":
                        if arg == 0:
                            dve.wait_ge(pv_free, NG * b)
                            after(dve, s_tlo, b - 1)
                            tail.start(b - 1)
                        softmax_out(arg, tail, osb, rec2[:, :], o2[:, :, :], rows["xbv"][:, :])
                    elif task in ("sturn", "nturn", "ttrans"):
                        dst, hi, lo, k = {"sturn": (turned, s_ghi, s_glo, n + 1), "nturn": (turned, s_nhi, s_nlo, n + 1),
                                          "ttrans": (oturned, s_thi, s_tlo, b)}[task]
                        dve.wait_ge(hi, k)
                        dve.tensor_tensor(dst[:, 1, :, 0:T], ps[:, bank, 0:C * T].rearrange("p (c t) -> p c t", t=T),
                                          dst[:, 0, :, 0:T], ALU.subtract).then_inc(lo, 1)
                    elif task == "tproj":
                        dve.wait_ge(pj_ready, ready)
                        dve.wait_ge(s_x1b, b)
                        after(dve, s_x2out, 16 * (b - 1))
                        dve.scalar_tensor_tensor(out=x2[:, :], in0=ps[0:T, bank, :], scalar=1.0 / WS,
                                                 in1=x1[:, it.npar], op0=ALU.mult, op1=ALU.add).then_inc(s_x2, 1)
                    elif task == "sscore":
                        dve.wait_ge(pj_ready, ready)
                        if arg == 0:
                            after(dve, s_slo, NG * n)
                        for j in range(GROUP):
                            h = GROUP * arg + j
                            ins = dve.scalar_tensor_tensor(out=sc[:, h], in0=keep.pd[:, :], scalar=keep.ld[:, bass.ds(n * H + h, 1)],
                                                           in1=ps[0:T, bank, j * T:(j + 1) * T], op0=ALU.mult, op1=ALU.add)
                        ins.then_inc(s_bias, 1)
                    elif task == "ssoft":
                        heads = slice(GROUP * arg, GROUP * (arg + 1))
                        dve.wait_ge(s_bias, NG * n + arg + 1)
                        dve.tensor_reduce(mx1[:, heads], sc[:, heads], AX.X, ALU.max).then_inc(s_smax, 1)
                        dve.wait_ge(s_smax, NG * n + arg + 1)
                        dve.tensor_tensor(sc[:, heads], sc[:, heads], mx1[:, heads, None].broadcast_to((T, GROUP, T)),
                                          ALU.subtract).then_inc(s_ssub, 1)
                    elif task == "strans":
                        dve.wait_ge(s_shi, NG * n + arg + 1)
                        dve.tensor_tensor(spl[:, arg % 2, :, 0:T], ps[0:T, bank, 0:GROUP * T].rearrange("p (h t) -> p h t", t=T),
                                          sph[:, arg % 2, :, 0:T], ALU.subtract).then_inc(s_slo, 1)
                    elif task == "sout":
                        dve.wait_ge(pj_ready, ready)
                        dve.tensor_copy(sraw[:, GROUP * arg:GROUP * (arg + 1)],
                                        ps[0:T, bank, 0:GROUP * VW].rearrange("p (h w) -> p h w", w=VW)).then_inc(s_sout, 1)
                    elif task == "snorm":
                        if arg == 0:
                            if is_first(n):
                                dve.wait_ge(s_const, 16 * 6)
                            dve.wait_ge(s_sout, NG * (n + 1))
                            norm.start(n)
                        softmax_out(arg, norm, sraw, small[:, 0], og[:, :, :], rows["bv"][:, :])
                        if arg == 1:
                            norm.step(dve.tensor_reduce(small[:, 1], og[:, :, :], AX.X, ALU.add))
                    elif task == "smean":
                        group.start(n)
                        dve.wait_ge(pj_ready, ready)
                        group.step(dve.tensor_copy(small[:, 2], ps[0:T, bank, 0:H]))
                        group.step(dve.tensor_tensor(og[:, :, :], og[:, :, :], spread(small[:, 2]), ALU.subtract))
                    elif task == "sdev":
                        group.step(dve.tensor_tensor(tmp[:, :, :], og[:, :, :], og[:, :, :], ALU.mult))
                        group.step(dve.tensor_reduce(small[:, 3], tmp[:, :, :], AX.X, ALU.add))
                    elif task == "svar":
                        dve.wait_ge(pj_ready, ready)
                        group.step(dve.tensor_scalar(small[:, 2], ps[0:T, bank, 0:H], EPS, None, ALU.add))
                        rsqrt_guess(dve, group, small[:, 4], small[:, 5], small[:, 2])
                    elif task == "snewton":
                        newton(dve, group, small[:, 4], small[:, 5], small[:, 2])
                        if arg == NEWTON - 1:
                            dve.tensor_tensor(og[:, :, :], og[:, :, :], spread(small[:, 4]), ALU.mult).then_inc(s_scaled, 1)
                    elif task == "sgate":
                        dve.wait_ge(s_affine, n + 1)
                        dve.wait_ge(s_self[3], 16 * (n + 1))
                        dve.scalar_tensor_tensor(out=ogf, in0=ogf, scalar=0.5, in1=gate[:, :], op0=ALU.mult,
                                                 op1=ALU.mult).then_inc(s_gated, 1)
                    elif task == "sproj":
                        dve.wait_ge(pj_ready, ready)
                        dve.wait_ge(s_xb, n + 1)
                        after(dve, s_x2, n - 1)
                        dve.scalar_tensor_tensor(out=x1[:, it.npar], in0=ps[0:T, bank, :], scalar=1.0 / WS,
                                                 in1=xr[:, :], op0=ALU.mult, op1=ALU.add).then_inc(s_x1, 1)
                        dve.wait_ge(s_x1, n + 1)
                        lnorm.start(n)
                        lnorm.step(dve.bn_stats(bn[:, :], x1[:, it.npar]))
                        dve.memset(ln[:, 2:3], 0.0)
                        lnorm.step(dve.bn_aggr(mv[:, :], bn[:, :]))
                        lnorm.step(dve.tensor_scalar(ln[:, 0:1], mv[:, 1:2], EPS, None, ALU.add))
                        rsqrt_guess(dve, lnorm, ln[:, 1:2], ln[:, 2:3], ln[:, 0:1])
                    elif task == "nnewton":
                        newton(dve, lnorm, ln[:, 1:2], ln[:, 2:3], ln[:, 0:1])
                        if arg < NEWTON - 1:
                            continue
                        dve.tensor_scalar(ogf, x1[:, it.npar], mv[:, 0:1], ln[:, 1:2], ALU.subtract,
                                          ALU.mult).then_inc(s_n2, 1)
                    elif task == "nproj":
                        for oc in range(C):
                            dve.wait_ge(s_q2hi, C * n + C)
                            ins = dve.scalar_tensor_tensor(out=q2[:, 1, oc], in0=ps[:, bank, oc * T:(oc + 1) * T],
                                                           scalar=cols[:, 2 * C + oc:2 * C + oc + 1], in1=q2[:, 0, oc],
                                                           op0=ALU.add, op1=ALU.subtract).then_inc(s_q2lo, 1)

            run(dve, body)

        def last_read(it, use):
            order = list(it.pj)
            b, n = it.b, it.n
            if use < 0:
                if is_first(n):
                    return s_init, 0
                order, b, n = before(it), b - 1, n - 1
            task, arg = order[use]
            return {"k": (s_klo, NKU * n + arg + 1), "v": (s_vlo, NVU * n + arg + 1), "sscore": (s_bias, NG * n + arg + 1),
                    "strans": (s_slo, NG * n + arg + 1), "sout": (s_sout, NG * n + arg + 1),
                    "smean": (s_mch, GROUP_STEPS * n + 1), "svar": (s_mch, GROUP_STEPS * n + 5),
                    "sturn": (s_glo, n + 1), "sproj": (s_x1, n + 1), "nturn": (s_nlo, n + 1), "nproj": (s_q2lo, C * n + C),
                    "ttrans": (s_tlo, b), "tproj": (s_x2, b)}[task]

        @block.tensor
        def _(pe):
            pe.wait_ge(s_initd, 5)

            def body(it):
                base, st_base, b, n = pj_base(it), FULL.st_n * it.b, it.b, it.n
                for task, arg in it.tasks:
                    use = it.pj.get((task, arg))
                    if use is not None:
                        bank = PJ + use % 2
                        s, value = last_read(it, use - 2)
                        after(pe, s, value)
                    if task == "k":
                        oc, hf = arg // 2, arg % 2
                        after(pe, s_clo, NCX * n)
                        passes(pe, ps[:, bank, 0:SH], lambda p, c: wb["xWk"][:, p, c, oc * P:(oc + 1) * P],
                               lambda p, c: ch[:, it.npar, p, c, hf * SH:(hf + 1) * SH]).then_inc(pj_ready, 1)
                    elif task == "v":
                        m = P if arg < KT - 1 else LASTK
                        after(pe, s_clo, NCX * n)
                        passes(pe, ps[0:m, bank, :], lambda p, c: ch[:, it.npar, p, c, arg * P:arg * P + m],
                               lambda p, c: wb["xWv"][:, p, c, :]).then_inc(pj_ready, 1)
                    elif task == "M":
                        if arg == 0:
                            if is_first(b):
                                pe.wait_ge(s_init, 4)
                        if arg < HPC:
                            pe.wait_ge(s_qst[arg], 16 * QST_DMAS * (b + 1))
                        if arg % (H // 2) == 0:
                            pe.wait_ge(s_kst[arg // (H // 2)], 16 * KST_DMAS * (b + 1))
                        after(pe, mx_done, H * b + arg)
                        for hf in range(2):
                            mm = pe.matmul(ps[:, MX + hf, 0:SH], qst[0:96, it.par, arg, :],
                                           kst[0:96, arg, hf * SH:(hf + 1) * SH], start=True, stop=True)
                        mm.then_inc(mx_ready, 1)
                    elif task == "W":
                        pe.wait_ge(w_ready, NG * b + arg + 1)
                        u = it.st[(task, arg)]
                        after(pe, st_free, st_base + u - 2)
                        for j in range(GROUP):
                            mm = pe.matmul(ps[:, ST + u % 3, j * T:(j + 1) * T], wrow[:, j, :], ident16[:, :],
                                           start=True, stop=True)
                        mm.then_inc(st_ready, 1)
                    elif task == "S":
                        pe.wait_ge(st_free, st_base + it.st[("W", arg // GROUP)] + 1)
                        for t in range(2):
                            u = it.st[(task, arg)] + t
                            after(pe, st_free, st_base + u - 2)
                            for k in range(KT // 2):
                                kt = t * KT // 2 + k
                                mm = pe.matmul(ps[:, ST + u % 3, k * T:(k + 1) * T], kst[:, arg, kt * P:(kt + 1) * P],
                                               qst[:, it.par, arg, 0:T], start=True, stop=True)
                            mm.then_inc(st_ready, 1)
                    elif task == "O":
                        if arg == 0:
                            pe.wait_ge(s_vlo, NVU * (b + 1))
                        if arg % GROUP == 0:
                            after(pe, pv_free, NG * b + arg // GROUP)
                        pe.wait_ge(s_pl, 2 * H * b + 2 * arg + 2)
                        out = ps[:, PV, (arg % GROUP) * VW:(arg % GROUP + 1) * VW]
                        for kt in range(KT):
                            m = P if kt < KT - 1 else LASTK
                            hi = lambda last: pe.matmul(out, ph[0:m, arg % 2, kt, :], v2[0:m, it.par, kt, arg, :],
                                                        start=(kt == 0), stop=last)
                            lo = lambda: pe.matmul(out[:, 0:HD + 1], pl[0:m, arg % 2, kt, :],
                                                   v2[0:m, it.par, kt, arg, 0:HD + 1], start=False, stop=False)
                            if kt < KT - 1:
                                hi(False)
                                lo()
                            else:
                                lo()
                                mm = hi(True)
                        mm.then_inc(pv_done, 1)
                    elif task == "sscore":
                        if arg == 0:
                            for s in s_self[0:2]:
                                pe.wait_ge(s, 16 * QK1_DMAS * (n + 1))
                        for j in range(GROUP):
                            h = GROUP * arg + j
                            mm = pe.matmul(ps[:, bank, j * T:(j + 1) * T], q1[0:96, h, :], k1[0:96, h, 0:T],
                                           start=True, stop=True)
                        mm.then_inc(pj_ready, 1)
                    elif task == "strans":
                        pe.wait_ge(s_sexp, NG * n + arg + 1)
                        for j in range(GROUP):
                            mm = pe.transpose(ps[0:T, bank, j * T:(j + 1) * T], sc[:, GROUP * arg + j, :], ident[0:T, 0:T])
                        mm.then_inc(pj_ready, 1)
                    elif task == "sout":
                        pe.wait_ge(s_slo, NG * n + arg + 1)
                        pe.wait_ge(s_self[2], 16 * (n + 1))
                        for j in range(GROUP):
                            h = GROUP * arg + j
                            out = ps[:, bank, j * VW:(j + 1) * VW]
                            pe.matmul(out, sph[:, arg % 2, j, :], v1[:, h, :], start=True, stop=False)
                            mm = pe.matmul(out[:, 0:HD + 1], spl[:, arg % 2, j, :], v1[:, h, 0:HD + 1], start=False, stop=True)
                        mm.then_inc(pj_ready, 1)
                    elif task == "smean":
                        pe.wait_ge(s_nch, NORM_STEPS * (n + 1))
                        pe.matmul(ps[:, bank, 0:H], mean_w[:, :], small[:, 1], start=True, stop=True).then_inc(pj_ready, 1)
                    elif task == "svar":
                        pe.wait_ge(s_mch, GROUP_STEPS * n + 4)
                        pe.matmul(ps[:, bank, 0:H], mean_w[:, :], small[:, 3], start=True, stop=True).then_inc(pj_ready, 1)
                    elif task in ("sturn", "nturn", "ttrans"):
                        src, s, k = {"sturn": (og, s_gated, n + 1), "nturn": (og, s_n2, n + 1), "ttrans": (o2, s_tch, TAIL_STEPS * b)}[task]
                        pe.wait_ge(s, k)
                        flat = src[:, :, :].rearrange("t h w -> t (h w)")
                        for c in range(C):
                            mm = pe.transpose(ps[:, bank, c * T:(c + 1) * T], flat[:, c * P:(c + 1) * P], ident[0:T, 0:T])
                        mm.then_inc(pj_ready, 1)
                    elif task in ("sproj", "tproj"):
                        src, w, s, k = {"sproj": (turned, "wo", s_glo, n + 1), "tproj": (oturned, "xWo", s_tlo, b)}[task]
                        pe.wait_ge(s, k)
                        passes(pe, ps[:, bank, :], lambda p, c: src[:, p, c, :], lambda p, c: wb[w][:, p, c, :]).then_inc(pj_ready, 1)
                    elif task == "nproj":
                        pe.wait_ge(s_nlo, n + 1)
                        for oc in range(C):
                            mm = passes(pe, ps[:, bank, oc * T:(oc + 1) * T], lambda p, c: wb["xWq"][:, p, c, oc * P:(oc + 1) * P],
                                        lambda p, c: turned[:, p, c, 0:T])
                        mm.then_inc(pj_ready, 1)

            run(pe, body)

WEIGHTS_C = ("base", "enc", "dec")
ADAPTER_DMAS = 4
NAD = 4


def phase_c(nc, d, keep):
    with ExitStack() as ctx:
        sb = lambda name, shape, dt: ctx.enter_context(nc.sbuf_tensor("c_" + name, shape, dt))
        sem = lambda name: ctx.enter_context(nc.semaphore("c_" + name))
        ps = ctx.enter_context(nc.psum_tensor("c_ps", [P, 8, 512], F32))
        EN, DE, MI = 0, 2, 6
        BA = (4, 5, 2, 3)
        NST = 3
        stage = sb("stage", [P, NST, C, E], F32)
        base = sb("base", [P, 2, C, E], F16)
        enc = sb("enc", [P, 2, NA, C, HID], F16)
        dec = sb("dec", [HID, 2, NA, E], F16)
        x = sb("x", [T, B, E], F32)
        ntok = sb("ntok", [T, 2, E], F32)
        nT = sb("nT", [P, 2, C, TOKP], F16)
        n32 = sb("n32", [P, C, TOK], F32)
        bnst = sb("bnst", [T, B, 6], F32)
        mv = sb("mv", [T, B, 2], F32)
        ve = sb("ve", [T, 3, B], F32)
        b_enc = sb("b_enc", [P, NA], F32)
        bbase = sb("bbase", [T, E], F32)
        h32 = sb("h32", [HID, 2, NT], F32)
        hhl = sb("hhl", [HID, 2, 2, NT], F16)
        err = sb("err", [P, 2, NT], F32)
        sq = sb("sq", [P, C, NT], F32)
        sqs = sb("sqs", [P, 2, NT], F32)
        loss = sb("loss", [P, NA, B], F32)
        ones = sb("ones", [P, P], F32)
        pick = sb("pick", [1, 8, NA * B], F32)
        iota = sb("iota", [1, NA], F32)
        conn = sb("conn", [1, NA], I32)
        connf = sb("connf", [1, NA], F32)
        sel = sb("sel", [1, B], I32)
        wd32 = sb("wd32", [P, NAD, C, R], F32)
        wdn = sb("wdn", [P, NAD, 2, C, R], F16)
        wu32 = sb("wu32", [R, NAD, E], F32)
        wup = sb("wup", [R, NAD, 2, E], F16)
        bdn = sb("bdn", [R, NAD, 1], F32)
        bup = sb("bup", [T, NAD, E], F32)
        mid32 = sb("mid32", [R, 2, T], F32)
        mid = sb("mid", [R, 2, 2, P], F16)
        res = sb("res", [T, 2, E], F32)

        s_x = [sem(f"x2_in{i}") for i in range(B // 2)]
        s_w = [sem(f"stage_in{i}") for i in range(NST)]
        s_const, s_init = sem("const_in"), sem("init")
        s_whi, s_wlo = sem("weights_hi"), sem("weights_lo")
        s_bn, s_mv, s_rs = sem("bn_stats"), sem("bn_aggr"), sem("rstd_chain")
        s_ntok, s_tp, s_nhi, s_nlo, s_n32 = sem("normed"), sem("transposed"), sem("nT_hi"), sem("nT_lo"), sem("nT_scaled")
        s_b = sem("bias")
        s_en, s_h32, s_hhi, s_hlo = sem("encoded"), sem("hidden"), sem("hidden_hi"), sem("hidden_lo")
        s_de, s_err, s_sq, s_sum, s_loss = sem("decoded"), sem("error"), sem("squares"), sem("square_sums"), sem("losses")
        s_tot, s_pick, s_sel = sem("loss_totals"), sem("pick_chain"), sem("adapter_chosen")
        s_ad = [sem(f"adapter_in{i}") for i in range(NAD)]
        s_xb = sem("x2_with_base_bias")
        s_adhi, s_adlo = sem("adapter_hi"), sem("adapter_lo")
        s_ba, s_mi, s_m32, s_mhi, s_mlo = sem("base_product"), sem("middle"), sem("middle_relu"), sem("middle_hi"), sem("middle_lo")
        s_up, s_pre, s_res = sem("adapter_product"), sem("residual_with_biases"), sem("result")
        s_out = [sem(f"stored{i}") for i in range(2)]
        block = ctx.enter_context(nc.Block())

        halves = lambda t: [t[:, :, 0:NA // 2], t[:, :, NA // 2:NA]]
        src_halves = lambda t: [t[:, 0:NA // 2], t[:, NA // 2:NA]]
        LOADS = [(src_halves(d["w"]["enc"])[0], halves(enc)[0]), (src_halves(d["w"]["dec"])[0], halves(dec)[0]),
                 (src_halves(d["w"]["enc"])[1], halves(enc)[1]), (src_halves(d["w"]["dec"])[1], halves(dec)[1]),
                 (d["w"]["base"], base)]
        NL = len(LOADS)
        ENC, DEC = (0, 2), (1, 3)
        UNITS = [(n, hf) for hf in range(2) for n in range(NA)]
        NU = len(UNITS)
        BESIDES = {0: (2, None), 1: (None, 4), 2: (3, 5), 3: (None, 6), 4: (None, 7), 7: (4, None)}
        assert max(u for u in BESIDES if BESIDES[u][1]) + 2 < NA - 1
        later = lambda u: BESIDES.get(u, (None, None))

        def staged(i):
            src = LOADS[i][0]
            flat = stage[:, i % NST].rearrange("p c e -> p (c e)")
            return flat if len(src.shape) == 2 else \
                flat.rearrange("p (a b) -> p a b", b=src.shape[2]) if len(src.shape) == 3 else \
                flat.rearrange("p (a b c) -> p a b c", b=src.shape[2], c=src.shape[3])

        @block.sync
        def _(sp):
            for i in range(B // 2):
                sp.dma_start(x[:, 2 * i:2 * i + 2], d["x2"][2 * i:2 * i + 2].rearrange("b t f -> t b f")).then_inc(s_x[i], 16)
            for i in range(NST):
                sp.dma_start(staged(i), LOADS[i][0]).then_inc(s_w[i], 16)
            sp.dma_start(bbase[:, :], d["rows"][7:8, :].broadcast_to((T, E))).then_inc(s_const, 16)
            sp.dma_start(conn[:, :], d["connected"]).then_inc(s_const, 16)
            sp.dma_start(iota[:, :], d["iota"]).then_inc(s_const, 16)
            for i in range(NST, NL):
                sp.wait_ge(s_wlo, i - NST + 1)
                sp.dma_start(staged(i), LOADS[i][0]).then_inc(s_w[i % NST], 16)

            def store(b):
                sp.wait_ge(s_res, b + 1)
                sp.dma_start(d["out"][b], res[:, b % 2]).then_inc(s_out[b % 2], 16)

            sp.wait_ge(s_sel, 1)
            for b in range(B):
                if b >= NAD:
                    sp.wait_ge(s_adlo, 2 * (b - NAD + 1))
                    sp.wait_ge(s_mhi, b - NAD + 1)
                    sp.wait_ge(s_pre, b - NAD + 1)
                a = sp.value_load(sel[0:1, b:b + 1], min_val=0, max_val=NA - 1)
                k = b % NAD
                for dst, src in ((wd32[:, k], d["w"]["down"]), (wu32[:, k], d["w"]["up"]), (bdn[:, k], d["b_down"])):
                    sp.dma_start(dst, src[a]).then_inc(s_ad[k], 16)
                sp.dma_start(bup[:, k], d["b_up"][bass.ds(a, 1), :].broadcast_to((T, E))).then_inc(s_ad[k], 16)
                if b >= NAD:
                    store(b - NAD)
            for b in range(B - NAD, B):
                store(b)
            for i in range(2):
                sp.wait_ge(s_out[i], 16 * (B // 2))

        @block.gpsimd
        def _(pool):
            pool.memset(nT[:, :, :, TOK:TOKP], 0.0).then_inc(s_init, 1)
            pool.memset(ones[:, :], 1.0).then_inc(s_init, 1)
            pool.memset(mid[:, :, :, T:P], 0.0).then_inc(s_init, 1)

            def hidden_lo(u):
                pool.wait_ge(s_hhi, u + 1)
                pool.tensor_tensor(hhl[:, u % 2, 1], h32[:, u % 2], hhl[:, u % 2, 0], ALU.subtract).then_inc(s_hlo, 1)

            def square_sums(u):
                for k in range(C - 1):
                    pool.wait_ge(s_sq, C * u + k + 2)
                    if k == 0 and u >= 2:
                        pool.wait_ge(s_loss, u - 1)
                    if k:
                        pool.wait_ge(s_sum, (C - 1) * u + k)
                    pool.tensor_tensor(sqs[:, u % 2], sqs[:, u % 2] if k else sq[:, 0], sq[:, k + 1],
                                       ALU.add).then_inc(s_sum, 1)

            def with_base_bias(b):
                pool.wait_ge(s_ntok, b + 1)
                pool.tensor_tensor(x[:, b], x[:, b], bbase[:, :], ALU.add).then_inc(s_xb, 1)

            for u in range(NU):
                hidden_lo(u)
                if u >= 1:
                    square_sums(u - 1)
            square_sums(NU - 1)
            pool.wait_ge(s_const, 48)
            for b in range(B):
                with_base_bias(b)

        @block.scalar
        def _(act):
            def weight_hi(i):
                act.wait_ge(s_w[i % NST], 16 * (i // NST + 1))
                act.activation(LOADS[i][1][:, 0], staged(i), ACT.Copy, scale=WS).then_inc(s_whi, 1)

            def turned_hi(b):
                act.wait_ge(s_tp, b + 1)
                act.activation(nT[:, 0, :, b * T:(b + 1) * T],
                               ps[:, MI + b % 2, 0:C * T].rearrange("p (c t) -> p c t", t=T), ACT.Copy).then_inc(s_nhi, 1)
                act.activation(n32[:, :, b * T:(b + 1) * T],
                               ps[:, MI + b % 2, 0:C * T].rearrange("p (c t) -> p c t", t=T), ACT.Copy, scale=WS).then_inc(s_n32, 1)

            weight_hi(0)
            weight_hi(1)
            for b in range(HALF):
                turned_hi(b)
            act.wait_ge(s_b, 1)

            def hidden(u):
                n, hf = UNITS[u]
                act.wait_ge(s_en, u + 1)
                if u >= 2:
                    act.wait_ge(s_hlo, u - 1)
                    act.wait_ge(s_de, C * (u - 1))
                act.activation(h32[:, u % 2], ps[:, EN + u % 2, 0:NT], ACT.Relu, bias=b_enc[:, n:n + 1],
                               scale=1.0 / WS).then_inc(s_h32, 1)
                act.wait_ge(s_h32, u + 1)
                act.activation(hhl[:, u % 2, 0], h32[:, u % 2], ACT.Copy).then_inc(s_hhi, 1)

            def squares(u):
                for oc in range(C):
                    i = C * u + oc
                    act.wait_ge(s_err, i + 1)
                    if u >= 1:
                        act.wait_ge(s_sum, (C - 1) * u)
                    act.activation(sq[:, oc], err[:, i % 2], ACT.Square, scale=1.0 / WS).then_inc(s_sq, 1)

            for u in range(NU):
                hidden(u)
                if u >= 1:
                    squares(u - 1)
                if later(u - 2)[1] is not None:
                    turned_hi(later(u - 2)[1])
                if later(u)[0] is not None:
                    weight_hi(later(u)[0])
            squares(NU - 1)

            def middle(b):
                act.wait_ge(s_mi, b + 1)
                if b >= 2:
                    act.wait_ge(s_up, b - 1)
                act.activation(mid32[:, b % 2], ps[0:R, MI + b % 2, 0:T], ACT.Relu, bias=bdn[:, b % NAD],
                               scale=1.0 / WS).then_inc(s_m32, 1)
                act.wait_ge(s_m32, b + 1)
                act.activation(mid[:, b % 2, 0, 0:T], mid32[:, b % 2], ACT.Copy).then_inc(s_mhi, 1)

            def adapter_hi(b):
                k = b % NAD
                act.wait_ge(s_ad[k], 16 * ADAPTER_DMAS * (b // NAD + 1))
                if b >= NAD:
                    act.wait_ge(s_up, b - NAD + 1)
                act.activation(wdn[:, k, 0], wd32[:, k], ACT.Copy, scale=WS).then_inc(s_adhi, 1)
                act.activation(wup[:, k, 0], wu32[:, k], ACT.Copy, scale=WS).then_inc(s_adhi, 1)

            adapter_hi(0)
            for b in range(B):
                if b + 1 < B:
                    adapter_hi(b + 1)
                middle(b)

        @block.vector
        def _(dve):
            chain = Chain(dve, s_rs, 1 + RSQRT_STEPS)

            def weight_lo(i):
                dve.wait_ge(s_whi, i + 1)
                dve.scalar_tensor_tensor(out=LOADS[i][1][:, 1], in0=staged(i), scalar=WS, in1=LOADS[i][1][:, 0],
                                         op0=ALU.mult, op1=ALU.subtract).then_inc(s_wlo, 1)

            def normed(b):
                if b >= 2:
                    dve.wait_ge(s_tp, b - 1)
                dve.tensor_scalar(ntok[:, b % 2], x[:, b], mv[:, b, 0:1], ve[:, 1, b:b + 1], ALU.subtract,
                                  ALU.mult).then_inc(s_ntok, 1)

            def lo(b):
                dve.wait_ge(s_n32, b + 1)
                dve.tensor_tensor(nT[:, 1, :, b * T:(b + 1) * T], ps[:, MI + b % 2, 0:C * T].rearrange("p (c t) -> p c t", t=T),
                                  nT[:, 0, :, b * T:(b + 1) * T], ALU.subtract).then_inc(s_nlo, 1)

            dve.tensor_scalar(b_enc[:, :], keep.cols[:, 4 * C:4 * C + NA], 1.0 / WS, None, ALU.mult).then_inc(s_b, 1)
            for b in range(B):
                dve.wait_ge(s_x[b // 2], 16)
                dve.bn_stats(bnst[:, b], x[:, b]).then_inc(s_bn, 1)
            for b in range(B):
                dve.wait_ge(s_bn, b + 1)
                dve.bn_aggr(mv[:, b], bnst[:, b]).then_inc(s_mv, 1)
            dve.wait_ge(s_mv, B)
            chain.start(0)
            chain.step(dve.tensor_scalar(ve[:, 0], mv[:, :, 1], EPS, None, ALU.add))
            rsqrt(dve, chain, ve[:, 1], ve[:, 2], ve[:, 0])
            for b in range(HALF):
                normed(b)
                if b == 0:
                    weight_lo(0)
                else:
                    lo(b - 1)
            lo(HALF - 1)
            weight_lo(1)

            def losses(u):
                n, hf = UNITS[u]
                dve.wait_ge(s_sum, (C - 1) * (u + 1))
                dve.tensor_reduce(loss[:, n, hf * HALF:(hf + 1) * HALF], sqs[:, u % 2].rearrange("p (b t) -> p b t", t=T),
                                  AX.X, ALU.add).then_inc(s_loss, 1)

            pc = Chain(dve, s_pick, 12)
            pc.start(0)
            v = lambda k: pick[:, k].rearrange("p (b n) -> p b n", n=NA)
            over_n = lambda t: t[:, :, None].broadcast_to((1, B, NA))
            over_b = lambda t: t[:, None, :].broadcast_to((1, B, NA))

            def numbers():
                neg = pick[:, 0, 0:NA]
                dve.wait_ge(s_const, 48)
                pc.step(dve.tensor_copy(connf[:, :], conn[:, :]))
                pc.step(dve.tensor_scalar(neg, connf[:, :], 0.0, float(NA), ALU.is_lt, ALU.mult))
                pc.step(dve.tensor_tensor(connf[:, :], connf[:, :], neg, ALU.add))
                pc.step(dve.tensor_scalar(connf[:, :], connf[:, :], 0.0, float(NA - 1), ALU.max, ALU.min))

            for u in range(NU):
                if u == NA:
                    numbers()
                n, hf = UNITS[u]
                for oc in range(C):
                    i = C * u + oc
                    dve.wait_ge(s_de, i + 1)
                    if i >= 2:
                        dve.wait_ge(s_sq, i - 1)
                    col = 4 * C + NA + n * C + oc
                    dve.scalar_tensor_tensor(out=err[:, i % 2], in0=ps[:, DE + i % 2, 0:NT], scalar=keep.cols[:, col:col + 1],
                                             in1=n32[:, oc, hf * NT:(hf + 1) * NT], op0=ALU.add,
                                             op1=ALU.subtract).then_inc(s_err, 1)
                if u >= 1:
                    losses(u - 1)
                if later(u - 2)[1] is not None:
                    lo(later(u - 2)[1])
                load, b = later(u)
                if b is not None:
                    normed(b)
                if load is not None:
                    weight_lo(load)
            losses(NU - 1)

            best = pick[:, 1, 0:B]
            dve.wait_ge(s_tot, 1)
            pc.step(dve.tensor_scalar(v(2), ps[0:1, EN, 0:NA * B].rearrange("p (n b) -> p b n", b=B), 1.0 / (T * E), None,
                                      ALU.mult))
            pc.step(dve.tensor_reduce(best, v(2), AX.X, ALU.min))
            pc.step(dve.tensor_tensor(v(3), v(2), over_n(best), ALU.is_gt))
            pc.step(dve.scalar_tensor_tensor(out=v(4), in0=v(3), scalar=float(NA), in1=over_b(iota[:, :]), op0=ALU.mult,
                                             op1=ALU.add))
            pc.step(dve.tensor_reduce(best, v(4), AX.X, ALU.min))
            pc.step(dve.tensor_tensor(v(5), over_b(iota[:, :]), over_n(best), ALU.is_equal))
            pc.step(dve.tensor_tensor(v(5), v(5), over_b(connf[:, :]), ALU.mult))
            pc.step(dve.tensor_reduce(best, v(5), AX.X, ALU.add))
            dve.tensor_copy(sel[:, :], best).then_inc(s_sel, 1)

            def finish(b):
                dve.wait_ge(s_up, b + 1)
                dve.wait_ge(s_pre, b + 1)
                if b >= 2:
                    dve.wait_ge(s_out[b % 2], 16 * (b // 2))
                dve.scalar_tensor_tensor(out=res[:, b % 2], in0=ps[0:T, BA[b % NAD], :], scalar=1.0 / WS, in1=x[:, b],
                                         op0=ALU.mult, op1=ALU.add).then_inc(s_res, 1)

            def middle_lo(b):
                dve.wait_ge(s_mhi, b + 1)
                dve.tensor_tensor(mid[:, b % 2, 1, 0:T], mid32[:, b % 2], mid[:, b % 2, 0, 0:T], ALU.subtract).then_inc(s_mlo, 1)

            dve.wait_ge(s_const, 48)
            def adapter_lo(b):
                k = b % NAD
                dve.wait_ge(s_adhi, 2 * b + 2)
                dve.scalar_tensor_tensor(out=wdn[:, k, 1], in0=wd32[:, k], scalar=WS, in1=wdn[:, k, 0],
                                         op0=ALU.mult, op1=ALU.subtract).then_inc(s_adlo, 1)
                dve.scalar_tensor_tensor(out=wup[:, k, 1], in0=wu32[:, k], scalar=WS, in1=wup[:, k, 0],
                                         op0=ALU.mult, op1=ALU.subtract).then_inc(s_adlo, 1)
                dve.wait_ge(s_xb, b + 1)
                dve.tensor_tensor(x[:, b], x[:, b], bup[:, k], ALU.add).then_inc(s_pre, 1)

            adapter_lo(0)
            for b in range(B + 1):
                if b + 1 < B:
                    adapter_lo(b + 1)
                if b < B:
                    middle_lo(b)
                if b >= 1:
                    finish(b - 1)

        @block.tensor
        def _(pe):
            def turn(b):
                pe.wait_ge(s_ntok, b + 1)
                if b >= 2:
                    pe.wait_ge(s_nlo, b - 1)
                for c in range(C):
                    mm = pe.transpose(ps[:, MI + b % 2, c * T:(c + 1) * T], ntok[:, b % 2, c * P:(c + 1) * P],
                                      keep.ident[0:T, 0:T])
                mm.then_inc(s_tp, 1)

            for b in range(HALF):
                turn(b)

            def encode(u):
                n, hf = UNITS[u]
                pe.wait_ge(s_wlo, ENC[n // (NA // 2)] + 1)
                pe.wait_ge(s_nlo, HALF * (hf + 1))
                if u >= 2:
                    pe.wait_ge(s_h32, u - 1)
                passes(pe, ps[:, EN + u % 2, 0:NT], lambda p, c: enc[:, p, n, c, :],
                       lambda p, c: nT[:, p, c, hf * NT:(hf + 1) * NT]).then_inc(s_en, 1)

            def decode(u):
                n, hf = UNITS[u]
                pe.wait_ge(s_wlo, DEC[n // (NA // 2)] + 1)
                pe.wait_ge(s_hlo, u + 1)
                for oc in range(C):
                    i = C * u + oc
                    if i >= 2:
                        pe.wait_ge(s_err, i - 1)
                    passes(pe, ps[:, DE + i % 2, 0:NT], lambda p, c: dec[:, p, n, oc * P:(oc + 1) * P],
                           lambda p, c: hhl[:, u % 2, p], chunks=1).then_inc(s_de, 1)

            def base_product(b):
                if b >= NAD:
                    pe.wait_ge(s_res, b - NAD + 1)
                elif BA[b] >= DE and BA[b] < DE + 2:
                    pe.wait_ge(s_err, C * NU)
                passes(pe, ps[:, BA[b % NAD], :], lambda p, c: nT[:, p, c, b * T:b * T + P], lambda p, c: base[:, p, c, :],
                       stop=False)

            encode(0)
            for u in range(NU):
                if u + 1 < NU:
                    encode(u + 1)
                decode(u)
                if later(u - 1)[1] is not None:
                    turn(later(u - 1)[1])
            pe.wait_ge(s_init, 3)
            pe.wait_ge(s_wlo, NL)
            base_product(0)
            base_product(1)
            pe.wait_ge(s_loss, NU)
            pe.matmul(ps[:, EN, 0:NA * B], ones[:, :], loss[:, :, :].rearrange("p n b -> p (n b)"),
                      start=True, stop=True).then_inc(s_tot, 1)
            for b in range(2, NAD):
                base_product(b)
            for b in range(B + 1):
                if b < B:
                    pe.wait_ge(s_adlo, 2 * b + 2)
                    if b >= 2:
                        pe.wait_ge(s_mhi, b - 1)
                    passes(pe, ps[0:R, MI + b % 2, 0:T], lambda p, c: wdn[:, b % NAD, p, c, :],
                           lambda p, c: nT[:, p, c, b * T:(b + 1) * T]).then_inc(s_mi, 1)
                if 2 <= b < B - NAD + 2:
                    base_product(b + NAD - 2)
                if b >= 1:
                    up = b - 1
                    pe.wait_ge(s_mlo, up + 1)
                    passes(pe, ps[:, BA[up % NAD], :], lambda p, c: mid[:, up % 2, p, :], lambda p, c: wup[:, up % NAD, p, :],
                           chunks=1, start=False).then_inc(s_up, 1)


def shapes_only_constants():
    inv_freq = (1.0 / 10000.0 ** (np.arange(0, HD, 2, dtype=np.float32) / np.float32(HD))).astype(np.float32)
    freqs = np.arange(T, dtype=np.float32)[:, None] * inv_freq[None, :]
    emb = np.concatenate([freqs, freqs], axis=-1)
    sign = np.where(np.arange(HD) % 2, 1.0, -1.0).astype(np.float32)
    cos = np.tile(np.cos(emb).T, (HPC, 1)).astype(np.float32)
    sin = np.tile((np.sin(emb) * sign).T, (HPC, 1)).astype(np.float32)
    at = np.arange(T, dtype=np.float32)
    return {"cos": cos, "sin": sin, "ident": np.eye(P, dtype=np.float32),
            "iota": np.arange(NA, dtype=np.float32).reshape(1, NA),
            "pos_diff": np.clip(at[None, :] - at[:, None], 0, None).astype(np.float32)}


def lay_out(a):
    on_partitions = lambda w: np.ascontiguousarray(w.reshape(C, P, -1).transpose(1, 0, 2))
    column = lambda v: v.reshape(-1, P).T
    f32 = {k: np.asarray(v) for k, v in a.items()}
    at, xa, ff = (lambda n: f32["L0_attn_" + n]), (lambda n: f32["L0_xattn_" + n]), (lambda n: f32["L0_ffn_" + n])
    out = {"x": f32["x"], **shapes_only_constants()}
    out["ctx"] = np.ascontiguousarray(f32["ctx_1024"].transpose(0, 2, 1).reshape(B, C, P, S))
    for w in WEIGHTS_A + ("wo",):
        out["w_" + w] = on_partitions(at(w).T)
    for w in ("Wq", "Wk", "Wv", "Wo"):
        out["w_x" + w] = on_partitions(xa(w).T)
    out["w_base"] = on_partitions(ff("W_base"))
    out["w_enc"] = np.ascontiguousarray(ff("W_enc").reshape(NA, C, P, HID).transpose(2, 0, 1, 3))
    out["w_dec"] = np.ascontiguousarray(ff("W_dec").transpose(1, 0, 2))
    out["w_down"] = np.ascontiguousarray(ff("W_down").reshape(NA, C, P, R).transpose(0, 2, 1, 3))
    out["w_up"] = ff("W_up")
    out["wd"] = on_partitions(at("wd").T)
    out["bd"] = at("bd").reshape(H, 1)
    out["rows"] = np.stack([at("bg"), at("gamma"), at("beta"), at("bo"), at("bv"), xa("bv"), xa("bo"), ff("b_base")])
    out["cols"] = np.ascontiguousarray(np.concatenate(
        [column(at("bq")), column(at("bk")), column(xa("bq")), column(xa("bk")), column(ff("b_enc")),
         column(ff("b_dec"))], axis=1))
    out["b_down"] = ff("b_down").reshape(NA, R, 1)
    out["b_up"] = ff("b_up")
    out["connected"] = ff("connected_idx").reshape(1, NA)
    return out


def scratch(nc, kind="Internal"):
    mk = lambda name, shape, dt: nc.dram_tensor(name, shape, dt, kind=kind).ap()
    return dict(q1=mk("q1", (2, E, TOK), F16), k1=mk("k1", (2, E, TOK), F16), v1=mk("v1", (B, T, H * VW), F16),
                gate=mk("gate", (B, T, E), F32), x2=mk("x2", (B, T, E), F32))


def build(nc, ins, scr, out, phases="abc"):
    d = {**ins, **scr, "out": out}
    d["w"] = {name[2:]: ap for name, ap in ins.items() if name[:2] == "w_"}
    with ExitStack() as ctx:
        sb = lambda name, shape, dt: ctx.enter_context(nc.sbuf_tensor(name, shape, dt))
        keep = Names()
        keep.ident = sb("ident", [P, P], F32)
        keep.pd = sb("pd", [T, T], F32)
        keep.cols = sb("cols", [P, NCOLS], F32)
        keep.ld = sb("ld", [T, B * H], F32)
        with ExitStack() as inner:
            keep.wb = {w: inner.enter_context(nc.sbuf_tensor("k_" + w, [P, 2, C, E], F16)) for w in WEIGHTS_B}
            keep.ch = inner.enter_context(nc.sbuf_tensor("k_ch", [P, 2, 2, C, S], F16))
            if "a" in phases:
                phase_a(nc, d, keep)
            if "b" in phases:
                phase_b(nc, d, keep)
        if "c" in phases:
            phase_c(nc, d, keep)


def kernel(**inputs):
    import concourse.bacc as bacc
    from concourse.bass_utils import run_bass_kernel_spmd

    arrays = {"in_" + k: v for k, v in lay_out(inputs).items()}
    nc = bacc.Bacc("TRN2", target_bir_lowering=False, num_devices=1)
    ins = {k[3:]: nc.dram_tensor(k, v.shape, mybir.dt.from_np(v.dtype), kind="ExternalInput").ap()
           for k, v in arrays.items()}
    out = nc.dram_tensor("out", (B, T, E), F32, kind="ExternalOutput").ap()
    build(nc, ins, scratch(nc), out)
    r = run_bass_kernel_spmd(nc, [arrays], core_ids=[0])
    return r.results[0]["out"]
```
